# Optimizing a Trainium2 kernel written in Bass

```python
import numpy as np
import jax
import jax.numpy as jnp

def _softmax(x, axis=-1):
    return jax.nn.softmax(x, axis=axis)

def _gelu(x):
    return jax.nn.gelu(x, approximate=True)

def _silu(x):
    return jax.nn.silu(x)

def _sigmoid(x):
    return jax.nn.sigmoid(x)

def _layernorm(x, axis=-1, eps=1e-05):
    m = jnp.mean(x, axis=axis, keepdims=True)
    v = jnp.var(x, axis=axis, keepdims=True)
    return (x - m) / jnp.sqrt(v + eps)

def _scatter_add(tgt, idx, src, axis=0):
    return tgt.at[idx].add(src)

def _segment_sum(src, seg, n):
    return jax.ops.segment_sum(src, seg, n)
kernel_name = 'mk_adj_resnorm_d2_adj_r2_cafb41'

def setup_inputs(seed: int=0):
    np.random.seed(seed)
    _w = jnp.asarray

    def _rec_inputs():
        import jax
        import jax.numpy as jnp
        _gk = jax.random.key(seed)
        x = -0.0003929 + 0.9999 * jax.random.normal(jax.random.fold_in(_gk, 1), (128, 128, 128), jnp.float32)
        _a = jax.random.bernoulli(jax.random.fold_in(_gk, 2), 0.0625, (128, 128))
        _a = jnp.logical_or(_a, jnp.swapaxes(_a, -1, -2))
        _a = jnp.logical_or(_a, jnp.eye(128, dtype=bool))
        _af = _a.astype(jnp.float32)
        _af = _af * jax.random.uniform(jax.random.fold_in(_gk, 3), (128, 128), jnp.float32, 0.05, 1)
        adj = _af
        return (x, adj)
    x, adj = _rec_inputs()

    def _L0_gnn_setup():
        import jax, jax.numpy as jnp
        import numpy as np
        EPS = 1e-05

        def _batchnorm(x, gamma, beta):
            mu = jnp.mean(x, axis=0)
            var = jnp.var(x, axis=0)
            return (x - mu) * jax.lax.rsqrt(var + EPS) * gamma + beta
        key = jax.random.key(seed)
        ks = jax.random.split(key, 4)
        b, n, d, h, o = (32, 1024, 128, 256, 128)
        features = jax.random.normal(ks[0], (b, n, d), dtype=jnp.float32)
        A = jax.random.uniform(ks[1], (n, n), dtype=jnp.float32)
        lim1 = float(np.sqrt(6.0 / (d + h)))
        W1 = jax.random.uniform(ks[2], (h, d), minval=-lim1, maxval=lim1, dtype=jnp.float32)
        b1 = jnp.zeros((h,), jnp.float32)
        lim2 = float(np.sqrt(6.0 / (h + o)))
        W2 = jax.random.uniform(ks[3], (o, h), minval=-lim2, maxval=lim2, dtype=jnp.float32)
        b2 = jnp.zeros((o,), jnp.float32)
        g1 = jnp.ones((h,), jnp.float32)
        be1 = jnp.zeros((h,), jnp.float32)
        g2 = jnp.ones((o,), jnp.float32)
        be2 = jnp.zeros((o,), jnp.float32)
        return {'features': features, 'A': A, 'W1': W1, 'b1': b1, 'g1': g1, 'be1': be1, 'W2': W2, 'b2': b2, 'g2': g2, 'be2': be2}
    _L0_gnn_all = _L0_gnn_setup()
    _L0_gnn_in = {k: v for k, v in _L0_gnn_all.items() if k in ('W1', 'b1', 'g1', 'be1', 'W2', 'b2', 'g2', 'be2')}
    del _L0_gnn_all

    def _L1_gnn_setup():
        import jax, jax.numpy as jnp
        import numpy as np
        B, T, D, H = (64, 1024, 128, 128)
        MAX_SKIP = 4

        def _lstm_last(Wih, Whh, bih, bhh, xs):
            N, _, Hd = xs.shape
            bias = bih + bhh

            def step(carry, x_t):
                h, c = carry
                g = x_t @ Wih.T + h @ Whh.T + bias
                i, f, gg, o = jnp.split(g, 4, axis=-1)
                c = jax.nn.sigmoid(f) * c + jax.nn.sigmoid(i) * jnp.tanh(gg)
                h = jax.nn.sigmoid(o) * jnp.tanh(c)
                return ((h, c), None)
            init = (jnp.zeros((N, Hd), xs.dtype), jnp.zeros((N, Hd), xs.dtype))
            (h_last, _), _ = jax.lax.scan(step, init, jnp.swapaxes(xs, 0, 1))
            return h_last
        key = jax.random.key(seed)
        ks = jax.random.split(key, 8)
        s = 0.05
        x = jax.random.normal(ks[0], (B, T, D), jnp.float32)
        adj = jax.random.uniform(ks[1], (T, T), jnp.float32) / T
        Wg0 = jax.random.normal(ks[2], (D, H), jnp.float32) * s
        bg0 = jnp.zeros((H,), jnp.float32)
        Wg1 = jax.random.normal(ks[3], (H, H), jnp.float32) * s
        bg1 = jnp.zeros((H,), jnp.float32)
        Wih = jax.random.normal(ks[4], (MAX_SKIP, 4 * H, H), jnp.float32) * s
        Whh = jax.random.normal(ks[5], (MAX_SKIP, 4 * H, H), jnp.float32) * s
        bih = jax.random.normal(ks[6], (MAX_SKIP, 4 * H), jnp.float32) * s
        bhh = jax.random.normal(ks[7], (MAX_SKIP, 4 * H), jnp.float32) * s
        return dict(x=x, adj=adj, Wg0=Wg0, bg0=bg0, Wg1=Wg1, bg1=bg1, Wih=Wih, Whh=Whh, bih=bih, bhh=bhh)
    _L1_gnn_all = _L1_gnn_setup()
    _L1_gnn_in = {k: v for k, v in _L1_gnn_all.items() if k in ('Wg0', 'bg0', 'Wg1', 'bg1', 'Wih', 'Whh', 'bih', 'bhh')}
    del _L1_gnn_all
    return {'x': x, 'adj': adj, 'L0_gnn_W1': _L0_gnn_in['W1'], 'L0_gnn_b1': _L0_gnn_in['b1'], 'L0_gnn_g1': _L0_gnn_in['g1'], 'L0_gnn_be1': _L0_gnn_in['be1'], 'L0_gnn_W2': _L0_gnn_in['W2'], 'L0_gnn_b2': _L0_gnn_in['b2'], 'L0_gnn_g2': _L0_gnn_in['g2'], 'L0_gnn_be2': _L0_gnn_in['be2'], 'L1_gnn_Wg0': _L1_gnn_in['Wg0'], 'L1_gnn_bg0': _L1_gnn_in['bg0'], 'L1_gnn_Wg1': _L1_gnn_in['Wg1'], 'L1_gnn_bg1': _L1_gnn_in['bg1'], 'L1_gnn_Wih': _L1_gnn_in['Wih'], 'L1_gnn_Whh': _L1_gnn_in['Whh'], 'L1_gnn_bih': _L1_gnn_in['bih'], 'L1_gnn_bhh': _L1_gnn_in['bhh']}

def reference(x, adj, L0_gnn_W1, L0_gnn_b1, L0_gnn_g1, L0_gnn_be1, L0_gnn_W2, L0_gnn_b2, L0_gnn_g2, L0_gnn_be2, L1_gnn_Wg0, L1_gnn_bg0, L1_gnn_Wg1, L1_gnn_bg1, L1_gnn_Wih, L1_gnn_Whh, L1_gnn_bih, L1_gnn_bhh):
    import jax
    import jax.numpy as jnp

    def _L0_gnn_ref(features, A, W1, b1, g1, be1, W2, b2, g2, be2):
        import jax, jax.numpy as jnp
        import numpy as np
        EPS = 1e-05

        def _batchnorm(x, gamma, beta):
            mu = jnp.mean(x, axis=0)
            var = jnp.var(x, axis=0)
            return (x - mu) * jax.lax.rsqrt(var + EPS) * gamma + beta
        b, n, d = features.shape
        A_norm = A + jnp.eye(n, dtype=A.dtype)
        deg = jnp.sum(A_norm, axis=0) + jnp.sum(A_norm, axis=1) - jnp.diagonal(A_norm)
        dinv = jax.lax.rsqrt(deg)
        A_hat = A_norm * dinv[:, None] * dinv[None, :]
        agg = jnp.einsum('nm,bmd->bnd', A_hat, features)
        x = agg.reshape(-1, d)
        h = jax.nn.relu(_batchnorm(x @ W1.T + b1, g1, be1))
        out = h @ W2.T + b2
        out = _batchnorm(out, g2, be2)
        return out.reshape(b, n, -1)

    def _L1_gnn_ref(x, adj, Wg0, bg0, Wg1, bg1, Wih, Whh, bih, bhh):
        import jax, jax.numpy as jnp
        import numpy as np
        B, T, D, H = (64, 1024, 128, 128)
        MAX_SKIP = 4

        def _lstm_last(Wih, Whh, bih, bhh, xs):
            N, _, Hd = xs.shape
            bias = bih + bhh

            def step(carry, x_t):
                h, c = carry
                g = x_t @ Wih.T + h @ Whh.T + bias
                i, f, gg, o = jnp.split(g, 4, axis=-1)
                c = jax.nn.sigmoid(f) * c + jax.nn.sigmoid(i) * jnp.tanh(gg)
                h = jax.nn.sigmoid(o) * jnp.tanh(c)
                return ((h, c), None)
            init = (jnp.zeros((N, Hd), xs.dtype), jnp.zeros((N, Hd), xs.dtype))
            (h_last, _), _ = jax.lax.scan(step, init, jnp.swapaxes(xs, 0, 1))
            return h_last
        h = jax.nn.relu(jnp.einsum('ts,bsh->bth', adj, x @ Wg0 + bg0))
        h = jax.nn.relu(jnp.einsum('ts,bsh->bth', adj, h @ Wg1 + bg1))
        Bv, Tv, Hd = h.shape
        for p in range(1, MAX_SKIP + 1):
            nw = Tv // p
            wins = h[:, :nw * p, :].reshape(Bv * nw, p, Hd)
            last = _lstm_last(Wih[p - 1], Whh[p - 1], bih[p - 1], bhh[p - 1], wins)
            idx = jnp.arange(nw) * p + (p - 1)
            h = h.at[:, idx, :].set(last.reshape(Bv, nw, Hd))
        return h
    x = _layernorm(x + _L0_gnn_ref(x, adj, L0_gnn_W1, L0_gnn_b1, L0_gnn_g1, L0_gnn_be1, L0_gnn_W2, L0_gnn_b2, L0_gnn_g2, L0_gnn_be2), axis=-1)
    x = _layernorm(x + _L1_gnn_ref(x, adj, L1_gnn_Wg0, L1_gnn_bg0, L1_gnn_Wg1, L1_gnn_bg1, L1_gnn_Wih, L1_gnn_Whh, L1_gnn_bih, L1_gnn_bhh), axis=-1)
    return x

_drawn_inputs = setup_inputs


def setup_inputs(seed=0):
    import zlib

    import numpy as np

    out = dict(_drawn_inputs(seed))
    spreads = {'L0_gnn_b1': (0.0, 0.8),
     'L0_gnn_g1': (1.0, 0.2),
     'L0_gnn_be1': (0.0, 0.1),
     'L0_gnn_b2': (0.0, 0.8),
     'L0_gnn_g2': (1.0, 0.2),
     'L0_gnn_be2': (0.0, 0.1),
     'L1_gnn_bg0': (0.0, 0.1),
     'L1_gnn_bg1': (0.0, 0.1)}
    factors = {'L1_gnn_Whh': 8.0, 'L1_gnn_bih': 2.976, 'L1_gnn_bhh': 3.011}
    for name, (base, spread) in spreads.items():
        noise = np.random.default_rng([zlib.crc32(name.encode()), seed]).standard_normal(out[name].shape)
        drawn = base * np.exp(spread * noise) if base else spread * noise
        out[name] = jnp.asarray(drawn.astype(out[name].dtype))
    for name, factor in factors.items():
        out[name] = (out[name] * factor).astype(out[name].dtype)
    return out
```

```python
from collections import namedtuple
from contextlib import ExitStack

import concourse.bass as bass
from concourse import mybir

F32 = mybir.dt.float32
F16 = mybir.dt.float16
ALU = mybir.AluOpType
ACT = mybir.ActivationFunctionType

P = 128
B = 128
HID = 256
HALVES = HID // P
COLS = B * P
CB = 4
CH = CB * P
CHUNKS = B // CB
UNROLL = 4
GB = 16
GC = GB * P
GCH = GB // CB
GROUPS = B // GB
EPS = 1e-5

WS = 64.0
HS = 256.0
MAX_SKIP = 4
WSL = MAX_SKIP * 4 * P // CHUNKS
GATE = {"i": 0, "f": 1, "g": 2, "o": 3}
BANK = {"i": 0, "g": 1, "f": 2, "o": 3}

Unit = namedtuple("Unit", "thread p s c b0 nb nw n k gate0")


def lstm_units(thread, plan):
    units, gate0 = [], 0
    for k, (p, s, c, b0, nb) in enumerate(plan):
        nw = P // p
        units.append(Unit(thread, p, s, c, b0, nb, nw, nb * nw, k, gate0))
        gate0 += 3 if s == 1 else 4
    return units, gate0


X_UNITS, X_GATES = lstm_units("x", [(1, 1, j, CB * j, CB) for j in range(GCH)]
                              + [(2, 1, c, 8 * c, 8) for c in range(2)]
                              + [(2, 2, c, 8 * c, 8) for c in range(2)])
Y_UNITS, Y_GATES = lstm_units("y", [(3, s, c, 8 * c, 8) for s in (1, 2, 3) for c in range(2)]
                              + [(4, s, 0, 0, GB) for s in (1, 2, 3, 4)])
NX, NY = len(X_UNITS), len(Y_UNITS)


def unit(p, s, c=0):
    return next(u for u in X_UNITS + Y_UNITS if (u.p, u.s, u.c) == (p, s, c))


def gates(u):
    return "igo" if u.s == 1 else "figo"


def gate_no(u, q):
    return u.gate0 + gates(u).index(q) + 1


ORDER = [("norm1", 0), ("norm1", 1), ("norm1", 2), ("norm1", 3), unit(3, 1, 0), ("pair", 0), ("pair", 1),
         unit(3, 1, 1), ("pair", 2), ("pair", 3), unit(3, 2, 0), ("agg1", 0), ("agg1", 1), unit(3, 2, 1), ("agg1", 2), ("agg1", 3),
         ("lin1", 0), ("lin1", 1), unit(3, 3, 0), ("lin1", 2), ("lin1", 3), ("lin2", 0), ("lin2", 1),
         unit(3, 3, 1), ("lin2", 2), ("lin2", 3), ("agg2", 0), ("agg2", 1), ("agg2", 2), ("agg2", 3),
         unit(4, 1), unit(1, 1, 0), unit(1, 1, 1), unit(4, 2), unit(1, 1, 2), unit(1, 1, 3),
         unit(2, 1, 0), unit(4, 3), unit(2, 1, 1), unit(2, 2, 0), unit(4, 4), unit(2, 2, 1),
         ("norm2", 0), ("norm2", 1), ("norm2", 2), ("norm2", 3),
         ("store", 0), ("store", 1), ("store", 2), ("store", 3)]


def thread_of(item):
    return item.thread if isinstance(item, Unit) else "y" if item[0] in ("norm2", "store") else "x"


def gnn_kernel(nc, xn, adj, adjT, W1T, W2T, vec1, vec2, Wg0, Wg1, bg0, bg1, WihT, WhhT, bih, bhh,
               consts, out):
    ctx = ExitStack()
    with ctx:
        def sb(name, shape, dt=F32):
            return ctx.enter_context(nc.sbuf_tensor(name, shape, dt))

        def sem(name):
            return ctx.enter_context(nc.semaphore(name))

        z = sb("z", [P, HALVES, COLS])
        late = z[:, 1, :]

        def carve(at, n, dt=F32):
            return late[:, at:at + n] if dt is F32 else late[:, at:at + n].bitcast(dt)

        x1 = carve(0, 2 * GC).rearrange("p (t c) -> p t c", t=2)
        opA = carve(4096, GC, F16).rearrange("p (l c) -> p l c", l=2)
        opB = carve(6144, GC, F16).rearrange("p (l c) -> p l c", l=2)
        H = carve(8192, 2 * GC, F16).rearrange("p (t l c) -> p t l c", t=2, l=2)
        xin = carve(12288, GCH * CH).rearrange("p (j c) -> p j c", j=GCH)
        yT = carve(14336, GCH * CH).rearrange("p (j c) -> p j c", j=GCH)

        gbuf = {t: sb(f"gbuf_{t}", [P, 2, 4, CH]) for t in "xy"}
        cell = {t: sb(f"cell_{t}", [P, 2, CH]) for t in "xy"}
        hst = {t: sb(f"hst_{t}", [P, 2, 2, CH], F16) for t in "xy"}
        wst = gbuf["x"][:, :, :, :].rearrange("p a q c -> p (a q c)").rearrange("p (m c) -> p m c", m=2)
        W = sb("W", [P, 2, 2, MAX_SKIP * 4 * P], F16)
        xa = gbuf["y"][:, :, :, :].rearrange("p a q c -> p (a q) c")
        x_ring, agg = xa[:, 0:4, :], xa[:, 4:6, :]
        w1 = sb("w1", [P, HID])
        w2 = sb("w2", [P, HALVES, P])
        v1 = sb("v1", [P, 3, HALVES])
        v2 = sb("v2", [P, 3])
        cst = sb("cst", [P, P + 8])
        ident = cst[:, 0:P]
        adj_n = sb("adj_n", [P, P])
        adj_t = sb("adj_t", [P, P])
        wg = sb("wg", [P, 2, P])
        bgr = sb("bgr", [P, 2, P])
        bi = sb("bi", [P, 2, MAX_SKIP * 4])
        gbias = sb("gbias", [P, MAX_SKIP * 4])
        ahat = sb("ahat", [P, P])
        adjh = sb("adjh", [P, 2, P], F16)
        wgh = sb("wgh", [P, 2, 2, P], F16)
        idh = sb("idh", [P, P], F16)
        bias1_w = sb("bias1_w", [P, P], F16)
        bias1_x = sb("bias1_x", [P, CB, P], F16)
        bias2_w = sb("bias2_w", [P, P], F16)
        bias2_x = sb("bias2_x", [P, CB, P], F16)
        early = cell["x"][:, :, :].rearrange("p a (q c) -> p (a q) c", c=P)
        tmp, ones, zero = early[:, 0:4, :], early[:, 4, :], early[:, 5, :]
        tmph = sb("tmph", [P, 2, P], F16)
        minus_half = sb("minus_half", [P, CB])
        sm = sb("sm", [P, 6])
        mark = sb("mark", [P, GCH + 2])
        stats1 = sb("stats1", [P, HALVES, CHUNKS, 6])
        stats2 = stats1[:, 0, :, :]
        mv1 = sb("mv1", [P, HALVES, 2])
        mv2 = sb("mv2", [P, 1, 2])
        bn1 = sb("bn1", [P, 4, HALVES])
        bn2 = sb("bn2", [P, 4, 1])
        lst = {t: sb(f"lst_{t}", [P, GCH, CB, 6]) for t in "xy"}
        lmv = {t: sb(f"lmv_{t}", [P, GCH, 5, CB]) for t in "xy"}
        lrs = {t: sb(f"lrs_{t}", [P, GCH, CB]) for t in "xy"}

        ps = ctx.enter_context(nc.psum_tensor("ps", [P, 8, CH], F32))
        bank0 = {"x": 0, "y": 4}

        ld_adj, ld_w1, ld_misc, ld_lstm = sem("ld_adj"), sem("ld_w1"), sem("ld_misc"), sem("ld_lstm")
        ld_x = [sem(f"ld_x{i}") for i in range(UNROLL)]
        ld_xin = [sem(f"ld_xin{i}") for i in range(GCH)]
        pre_d, pre_a, pre_p, pre_t = sem("pre_d"), sem("pre_a"), sem("pre_p"), sem("pre_t")
        w_hi, w_lo = sem("w_hi"), sem("w_lo")
        agg_mm, agg_cp = sem("agg_mm"), sem("agg_cp")
        z_mm, z_cp, z_st = sem("z_mm"), sem("z_cp"), sem("z_st")
        bn1_d, bn1_p = sem("bn1_d"), sem("bn1_p")
        r_act, o_mm, o_cp, o_st = sem("r_act"), sem("o_mm"), sem("o_cp"), sem("o_st")
        bn2_d, bn2_p = sem("bn2_d"), sem("bn2_p")
        yT_a, tr_t, y_d, st_d, mv_d, rs_p, x1_d, x1h_a, x1l_p = (
            sem(n) for n in ("yT_a", "tr_t", "y_d", "st_d", "mv_d", "rs_p", "x1_d", "x1h_a", "x1l_p"))
        agg1_t, lin1_t, lin2_t, agg2_t = (sem(n) for n in ("agg1_t", "lin1_t", "lin2_t", "agg2_t"))
        vh_a, rh_a, sh_a, h0h_a = (sem(n) for n in ("vh_a", "rh_a", "sh_a", "h0h_a"))
        vl_d, rl_d, sl_d, h0l_d = (sem(n) for n in ("vl_d", "rl_d", "sl_d", "h0l_d"))
        fin_t, y2_d, st2_d, mv2_d, rs2_p, o_d = (
            sem(n) for n in ("fin_t", "y2_d", "st2_d", "mv2_d", "rs2_p", "o_d"))
        stored = [sem(f"stored{j}") for j in range(GCH)]
        g_t = {t: sem(f"g_t_{t}") for t in "xy"}
        g_a = {t: sem(f"g_a_{t}") for t in "xy"}
        ig_d = {t: sem(f"ig_d_{t}") for t in "xy"}
        fc_p = {t: sem(f"fc_p_{t}") for t in "xy"}
        c_d = {t: sem(f"c_d_{t}") for t in "xy"}
        tc_a = {t: sem(f"tc_a_{t}") for t in "xy"}
        h_d = {t: sem(f"h_d_{t}") for t in "xy"}
        hi_d = {t: sem(f"hi_d_{t}") for t in "xy"}
        lo_p = {t: sem(f"lo_p_{t}") for t in "xy"}

        UNITS = {"x": NX, "y": NY}
        NGATES = {"x": X_GATES, "y": Y_GATES}
        F_PER_GROUP = {"x": 2, "y": 7}

        def chunk_no(g, j):
            return g * GCH + (j + 1)

        def unit_no(g, u):
            return g * UNITS[u.thread] + (u.k + 1)

        def gate_count(g, u, q):
            return g * NGATES[u.thread] + gate_no(u, q)

        def f_no(g, u):
            units = X_UNITS if u.thread == "x" else Y_UNITS
            return g * F_PER_GROUP[u.thread] + sum(w.s > 1 for w in units[:u.k + 1])

        def before(u):
            return (X_UNITS if u.thread == "x" else Y_UNITS)[u.k - 1]

        def cols(j):
            return slice(j * CH, (j + 1) * CH)

        def windows(hp, u, t):
            v = hp.rearrange("p (b t) -> p b t", t=P)
            return v[:, u.b0:u.b0 + u.nb, t:t + u.p * (u.nw - 1) + 1:u.p]

        def folded(ap, u):
            return ap.rearrange("p (b w) -> p b w", w=u.nw)

        def gate_buf(u, q):
            return gbuf[u.thread][:, u.k % 2, BANK[q], 0:u.n]

        def h_out(g, u, part):
            if u.s == u.p:
                return windows(H[:, g % 2, part, :], u, u.p - 1)
            return folded(hst[u.thread][:, u.c, part, 0:u.n], u)

        block = ctx.enter_context(nc.Block())

        def turns(eng, body):
            body(0, None)
            with eng.Fori(1, GROUPS) as g:
                body(g, g - 1)
            body(None, GROUPS - 1)

        @block.sync
        def _(sp):
            for dst, src in ((adj_n[:], adj), (adj_t[:], adjT), (cst[:], consts)):
                sp.dma_start(dst, src).then_inc(ld_adj, 16)
            sp.dma_start(w1[:], W1T).then_inc(ld_w1, 16)
            for i in range(UNROLL):
                sp.dma_start(x_ring[:, i, :], xn[:, cols(i)]).then_inc(ld_x[i], 16)
            for dst, src in ((v1[:], vec1), (v2[:], vec2), (w2[:], W2T), (wg[:, 0, :], Wg0), (wg[:, 1, :], Wg1),
                             (bgr[:, 0, :], bg0), (bgr[:, 1, :], bg1), (bi[:, 0, :], bih), (bi[:, 1, :], bhh)):
                sp.dma_start(dst, src).then_inc(ld_misc, 16)
            sp.dma_start(wst[:, 0, :], WihT).then_inc(ld_lstm, 16)
            sp.dma_start(wst[:, 1, :], WhhT).then_inc(ld_lstm, 16)
            with sp.Fori(1, CHUNKS // UNROLL) as n:
                for i in range(UNROLL):
                    sp.wait_ge(agg_mm, (n - 1) * UNROLL + (i + 1))
                    sp.dma_start(x_ring[:, i, :], xn[:, bass.ds(n * (UNROLL * CH) + i * CH, CH)]).then_inc(ld_x[i], 16)

            sp.wait_ge(o_mm, CHUNKS)
            for j in range(GCH):
                sp.dma_start(xin[:, j, :], xn[:, cols(j)]).then_inc(ld_xin[j], 16)

            def stores(gy):
                for item in ORDER:
                    if isinstance(item, Unit):
                        continue
                    kind, j = item
                    if kind == "store":
                        sp.wait_ge(o_d, gy * GCH + (GCH + j + 1))
                        sp.dma_start(out[:, bass.ds(gy * GC + j * CH, CH)], x1[:, gy % 2, cols(j)]).then_inc(stored[j], 16)

            def prefetch(g):
                for j in range(GCH):
                    sp.wait_ge(x1_d, chunk_no(g, j))
                    sp.dma_start(xin[:, j, :], xn[:, bass.ds(g * GC + (GC + j * CH), CH)]).then_inc(ld_xin[j], 16)

            prefetch(0)
            with sp.Fori(1, GROUPS - 1) as g:
                prefetch(g)
                stores(g - 1)
            stores(GROUPS - 2)
            stores(GROUPS - 1)
            for j in range(GCH):
                sp.wait_ge(stored[j], 16 * (GROUPS + 1))

        @block.tensor
        def _(pe):
            def mm(o, w, m, start, stop):
                return pe.matmul(o, w, m, start=start, stop=stop, skip_group_check=True)

            pe.wait_ge(ld_adj, 48)
            pe.wait_ge(pre_p, 2)
            mm(ps[:, 1, 0:P], ones, adj_t[:], True, True).then_inc(pre_t, 1)
            pe.wait_ge(pre_d, 6)
            pe.transpose(ps[:, 0, 0:P], tmp[:, 1, :], ident).then_inc(pre_t, 1)
            pe.wait_ge(pre_d, 8)
            pe.wait_ge(ld_w1, 16)

            def aggregate(n, i):
                k = n * UNROLL + i
                pe.wait_ge(ld_x[i], n * 16 + 16)
                if not (isinstance(k, int) and k < 2):
                    pe.wait_ge(agg_cp, k - 1)
                for b in range(CB):
                    last = mm(ps[:, i % 2, b * P:(b + 1) * P], x_ring[:, i, b * P:(b + 1) * P], ahat[:], True, True)
                last.then_inc(agg_mm, 1)

            def hidden(n, i):
                k = n * UNROLL + i
                pe.wait_ge(agg_cp, k + 1)
                if not (isinstance(k, int) and k < 2):
                    pe.wait_ge(z_cp, k - 1)
                for h in range(HALVES):
                    last = mm(ps[:, 2 + 2 * (i % 2) + h, :], w1[:, h * P:(h + 1) * P], agg[:, i % 2, :], True, True)
                last.then_inc(z_mm, 1)

            def turn_a(n):
                aggregate(n, 0)
                for i in range(1, UNROLL):
                    aggregate(n, i)
                    hidden(n, i - 1)
                hidden(n, UNROLL - 1)

            turn_a(0)
            with pe.Fori(1, CHUNKS // UNROLL) as n:
                turn_a(n)

            def turn_b(n):
                for i in range(UNROLL):
                    k = n * UNROLL + i
                    if not isinstance(n, int):
                        pe.wait_ge(o_cp, k - (UNROLL - 1))
                    pe.wait_ge(r_act, k + 1)
                    for h in range(HALVES):
                        last = mm(ps[:, i, :], w2[:, h, :], z[:, h, bass.ds(n * (UNROLL * CH) + i * CH, CH)],
                                  h == 0, h == HALVES - 1)
                    last.then_inc(o_mm, 1)

            pe.wait_ge(ld_misc, 144)
            pe.wait_ge(z_cp, CHUNKS)
            turn_b(0)
            with pe.Fori(1, CHUNKS // UNROLL) as n:
                turn_b(n)

            pe.wait_ge(o_cp, CHUNKS)
            pe.wait_ge(w_lo, CHUNKS)

            def node_products(o, stat, mov, j, first):
                for b in range(CB):
                    at = slice(j * CH + b * P, j * CH + (b + 1) * P)
                    mm(o[:, b * P:(b + 1) * P], stat[:, 0, at], mov[:, 0, :], first, False)
                    mm(o[:, b * P:(b + 1) * P], stat[:, 0, at], mov[:, 1, :], False, False)
                    last = mm(o[:, b * P:(b + 1) * P], stat[:, 1, at], mov[:, 0, :], False, True)
                return last

            def lstm(g, u):
                t, bank, prev = u.thread, bank0[u.thread], before(u)
                if u == unit(1, 1, 0):
                    pe.wait_ge(h0l_d, chunk_no(g, GCH - 1))
                elif u.p == 1:
                    pe.wait_ge(h0l_d, chunk_no(g, u.c))
                elif u.p == 2 and u.s == 1:
                    pe.wait_ge(lo_p["x"], unit_no(g, unit(1, 1, 2 * u.c + 1)))
                elif u.p == 3 and u.s == 1:
                    pe.wait_ge(lo_p["x"], unit_no(g, unit(2, 2, u.c)))
                    if u.c == 0:
                        pe.wait_ge(y2_d, g * GCH + GCH)
                elif u.p == 4 and u.s == 1:
                    pe.wait_ge(lo_p["y"], unit_no(g, unit(3, 3, 1)))
                src = opA if u.p == 1 else H[:, g % 2, :, :]
                for q in gates(u):
                    if u.k and q in gates(prev):
                        pe.wait_ge(g_a[t], gate_count(g, prev, q))
                    o = ps[:, bank + BANK[q], 0:u.n]
                    at = (u.p - 1) * 4 * P + GATE[q] * P
                    w = [W[:, 0, part, at:at + P] for part in range(2)]
                    x = [windows(src[:, part, :], u, u.s - 1) for part in range(2)]
                    mm(o, w[0], x[0], True, False)
                    mm(o, w[1], x[0], False, False)
                    last = mm(o, w[0], x[1], False, u.s == 1)
                    if u.s == 1:
                        last.then_inc(g_t[t], 1)
                if u.s == 1:
                    return
                pe.wait_ge(hi_d[t], unit_no(g, unit(u.p, u.s - 1, u.c)))
                for n, q in enumerate(gates(u)):
                    o = ps[:, bank + BANK[q], 0:u.n]
                    at = (u.p - 1) * 4 * P + GATE[q] * P
                    w = [W[:, 1, part, at:at + P] for part in range(2)]
                    h = [hst[t][:, u.c, part, 0:u.n] for part in range(2)]
                    mm(o, w[0], h[0], False, False)
                    mm(o, w[1], h[0], False, False)
                    if n == 0:
                        pe.wait_ge(lo_p[t], unit_no(g, unit(u.p, u.s - 1, u.c)))
                    mm(o, w[0], h[1], False, True).then_inc(g_t[t], 1)

            def turn_c(gx, gy):
                for item in ORDER:
                    g = gx if thread_of(item) == "x" else gy
                    if g is None:
                        continue
                    if isinstance(item, Unit):
                        lstm(g, item)
                        continue
                    kind, j = item
                    o = ps[:, j, :]
                    if kind == "norm1":
                        if not isinstance(g, int):
                            pe.wait_ge(g_a["x"], g * X_GATES)
                        pe.wait_ge(yT_a, chunk_no(g, j))
                        for b in range(CB):
                            last = pe.transpose(o[:, b * P:(b + 1) * P], yT[:, j, b * P:(b + 1) * P], ident)
                        last.then_inc(tr_t, 1)
                    elif kind == "agg1":
                        pe.wait_ge(x1h_a, chunk_no(g, j))
                        pe.wait_ge(x1l_p, chunk_no(g, j))
                        node_products(o, opA, adjh, j, True).then_inc(agg1_t, 1)
                    elif kind == "lin1":
                        pe.wait_ge(vl_d, chunk_no(g, j))
                        mm(o, bias1_w[:], bias1_x[:, :, :].rearrange("p b c -> p (b c)"), True, False)
                        mm(o, wgh[:, 0, 0, :], opB[:, 0, cols(j)], False, False)
                        mm(o, wgh[:, 0, 1, :], opB[:, 0, cols(j)], False, False)
                        mm(o, wgh[:, 0, 0, :], opB[:, 1, cols(j)], False, True).then_inc(lin1_t, 1)
                    elif kind == "lin2":
                        pe.wait_ge(rl_d, chunk_no(g, j))
                        mm(o, bias2_w[:], bias2_x[:, :, :].rearrange("p b c -> p (b c)"), True, False)
                        node_products(o, opA, wgh[:, 1, :, :], j, False).then_inc(lin2_t, 1)
                    elif kind == "agg2":
                        pe.wait_ge(sl_d, chunk_no(g, j))
                        node_products(o, opB, adjh, j, True).then_inc(agg2_t, 1)
                    elif kind == "norm2":
                        o = ps[:, bank0["y"] + j, :]
                        if j == 0:
                            pe.wait_ge(lo_p["y"], unit_no(g, unit(4, 4)))
                        for b in range(CB):
                            at = slice(j * CH + b * P, j * CH + (b + 1) * P)
                            mm(o[:, b * P:(b + 1) * P], H[:, g % 2, 0, at], idh[:], True, False)
                            last = mm(o[:, b * P:(b + 1) * P], H[:, g % 2, 1, at], idh[:], False, True)
                        last.then_inc(fin_t, 1)

            turns(pe, turn_c)

        @block.scalar
        def _(act):
            a = nc.scalar.activation

            act.wait_ge(ld_adj, 48)
            a(adjh[:, 0, :], adj_t[:], ACT.Copy, scale=WS).then_inc(pre_a, 1)
            act.wait_ge(ld_misc, 144)
            a(wgh[:, :, 0, :], wg[:], ACT.Copy, scale=WS).then_inc(pre_a, 1)
            a(idh[:], ident, ACT.Copy, scale=1.0 / HS).then_inc(pre_a, 1)

            def turn_a(n):
                for step in range(UNROLL + 1):
                    if step < UNROLL:
                        i = step
                        k = n * UNROLL + i
                        act.wait_ge(agg_mm, k + 1)
                        if not (isinstance(k, int) and k < 2):
                            act.wait_ge(z_mm, k - 1)
                        a(agg[:, i % 2, :], ps[:, i % 2, :], ACT.Copy).then_inc(agg_cp, 1)
                    if step:
                        i = step - 1
                        k = n * UNROLL + i
                        act.wait_ge(z_mm, k + 1)
                        a(z[:, :, bass.ds(n * (UNROLL * CH) + i * CH, CH)],
                          ps[:, 2 + 2 * (i % 2):4 + 2 * (i % 2), :], ACT.Copy).then_inc(z_cp, 1)
                        if isinstance(n, int) and step == 1:
                            act.wait_ge(ld_lstm, 32)
                        s = bass.ds(n * (UNROLL * WSL) + i * WSL, WSL)
                        a(W[:, :, 0, s], wst[:, :, s], ACT.Copy, scale=WS).then_inc(w_hi, 1)

            turn_a(0)
            with act.Fori(1, CHUNKS // UNROLL) as n:
                turn_a(n)

            act.wait_ge(bn1_d, 7)
            with act.Fori(0, CHUNKS // UNROLL) as n:
                for i in range(UNROLL):
                    for h in range(HALVES):
                        at = z[:, h, bass.ds(n * (UNROLL * CH) + i * CH, CH)]
                        last = a(at, at, ACT.Relu, bias=bn1[:, 3, h:h + 1], scale=bn1[:, 2, h:h + 1])
                    last.then_inc(r_act, 1)

            act.wait_ge(bn2_d, 7)

            def lstm(g, u):
                t = u.thread
                if u.k >= 2:
                    act.wait_ge(lo_p[t], g * UNITS[t] + (u.k - 1))
                scale = 1.0 / (WS * (WS if u.p == 1 else HS))
                for q in gates(u):
                    act.wait_ge(g_t[t], gate_count(g, u, q))
                    at = (u.p - 1) * 4 + GATE[q]
                    a(gate_buf(u, q), ps[:, bank0[t] + BANK[q], 0:u.n], ACT.Tanh if q == "g" else ACT.Sigmoid,
                      bias=gbias[:, at:at + 1], scale=scale).then_inc(g_a[t], 1)
                act.wait_ge(c_d[t], unit_no(g, u))
                a(gate_buf(u, "i"), cell[t][:, u.c % 2, 0:u.n], ACT.Tanh).then_inc(tc_a[t], 1)

            def turn_c(gx, gy):
                for item in ORDER:
                    g = gx if thread_of(item) == "x" else gy
                    if g is None:
                        continue
                    if isinstance(item, Unit):
                        lstm(g, item)
                        continue
                    kind, j = item
                    if kind == "norm1":
                        if not isinstance(g, int):
                            act.wait_ge(o_d, g * GCH - (GCH - 1) + j)
                        a(yT[:, j, :], z[:, 0, bass.ds(g * GC + j * CH, CH)], ACT.Identity,
                          bias=bn2[:, 3, 0:1], scale=bn2[:, 2, 0:1]).then_inc(yT_a, 1)
                    elif kind == "pair":
                        act.wait_ge(x1_d, chunk_no(g, j))
                        a(opA[:, 0, cols(j)], x1[:, g % 2, cols(j)], ACT.Copy).then_inc(x1h_a, 1)
                    elif kind == "agg1":
                        act.wait_ge(agg1_t, chunk_no(g, j))
                        a(opB[:, 0, cols(j)], ps[:, j, :], ACT.Copy, scale=1.0 / WS).then_inc(vh_a, 1)
                    elif kind == "lin1":
                        act.wait_ge(lin1_t, chunk_no(g, j))
                        a(opA[:, 0, cols(j)], ps[:, j, :], ACT.Relu).then_inc(rh_a, 1)
                    elif kind == "lin2":
                        act.wait_ge(lin2_t, chunk_no(g, j))
                        a(opB[:, 0, cols(j)], ps[:, j, :], ACT.Copy, scale=1.0 / (WS * WS)).then_inc(sh_a, 1)
                    elif kind == "agg2":
                        act.wait_ge(agg2_t, chunk_no(g, j))
                        a(opA[:, 0, cols(j)], ps[:, j, :], ACT.Relu).then_inc(h0h_a, 1)

            turns(act, turn_c)

        @block.vector
        def _(dve):
            v = nc.vector

            dve.wait_ge(ld_adj, 48)
            v.tensor_tensor(tmp[:, 0, :], adj_n[:], ident, ALU.add).then_inc(pre_d, 1)
            v.tensor_tensor(tmp[:, 2, :], adj_t[:], ident, ALU.add).then_inc(pre_d, 1)
            dve.wait_ge(pre_d, 2)
            v.reduce_sum(sm[:, 0:1], tmp[:, 0, :], mybir.AxisListType.X)
            v.reduce_sum(sm[:, 1:2], tmp[:, 2, :], mybir.AxisListType.X)
            v.tensor_tensor(tmp[:, 3, :], tmp[:, 0, :], ident, ALU.mult).then_inc(pre_d, 1)
            dve.wait_ge(pre_d, 3)
            v.reduce_sum(sm[:, 2:3], tmp[:, 3, :], mybir.AxisListType.X)
            v.tensor_tensor(sm[:, 3:4], sm[:, 0:1], sm[:, 1:2], ALU.add).then_inc(pre_d, 1)
            dve.wait_ge(pre_d, 4)
            v.tensor_tensor(sm[:, 4:5], sm[:, 3:4], sm[:, 2:3], ALU.subtract).then_inc(pre_d, 1)
            dve.wait_ge(pre_p, 3)
            v.tensor_scalar(tmp[:, 1, :], tmp[:, 0, :], sm[:, 5:6], None, ALU.mult).then_inc(pre_d, 1)
            dve.wait_ge(pre_t, 2)
            v.tensor_scalar(ahat[:], ps[:, 0, 0:P], sm[:, 5:6], None, ALU.mult).then_inc(pre_d, 1)

            def low(o, full, high, scale):
                return v.scalar_tensor_tensor(out=o, in0=full, scalar=scale, in1=high, op0=ALU.mult, op1=ALU.subtract)

            dve.wait_ge(pre_a, 1)
            low(adjh[:, 1, :], adj_t[:], adjh[:, 0, :], WS)
            pick = cst[:, P:P + 8]
            v.tensor_copy(tmp[:, 0, :], ps[:, 1, 0:P]).then_inc(pre_d, 1)
            dve.wait_ge(ld_misc, 144)
            v.tensor_scalar(tmp[:, 1, :], bgr[:, 0, :], WS, None, ALU.mult).then_inc(pre_d, 1)
            v.tensor_scalar(tmp[:, 2, :], bgr[:, 1, :], WS, None, ALU.mult).then_inc(pre_d, 1)
            v.tensor_tensor(gbias[:], bi[:, 0, :], bi[:, 1, :], ALU.add)
            at, done = 10, 10
            for src, dst, ph, pl, rep in ((tmp[:, 0, :], bias1_x, 0, 1, CB), (tmp[:, 1, :], bias1_w, 2, 3, 1),
                                          (tmp[:, 2, :], bias2_x, 4, 5, CB)):
                dve.wait_ge(pre_d, done)
                v.tensor_copy(tmph[:, 0, :], src).then_inc(pre_d, 1)
                dve.wait_ge(pre_d, done + 1)
                v.tensor_tensor(tmph[:, 1, :], src, tmph[:, 0, :], ALU.subtract).then_inc(pre_d, 1)
                v.tensor_scalar(tmp[:, 3, :], tmph[:, 0, :], pick[:, ph:ph + 1], None, ALU.mult).then_inc(pre_d, 1)
                dve.wait_ge(pre_d, done + 3)
                for b in range(rep):
                    o = dst[:, b, :] if rep > 1 else dst[:]
                    last = v.scalar_tensor_tensor(out=o, in0=tmph[:, 1, :], scalar=pick[:, pl:pl + 1],
                                                  in1=tmp[:, 3, :], op0=ALU.mult, op1=ALU.add)
                last.then_inc(pre_d, 1)
                done += 4
            dve.wait_ge(pre_p, 3)
            v.tensor_scalar(bias2_w[:], zero, pick[:, 6:7], WS, ALU.add, ALU.mult)
            dve.wait_ge(pre_a, 2)
            low(wgh[:, :, 1, :], wg[:], wgh[:, :, 0, :], WS)

            def turn_a(n):
                for i in range(UNROLL):
                    dve.wait_ge(w_hi, n * UNROLL + (i + 1))
                    dve.wait_ge(z_cp, n * UNROLL + (i + 1))
                    s = bass.ds(n * (UNROLL * WSL) + i * WSL, WSL)
                    low(W[:, :, 1, s], wst[:, :, s], W[:, :, 0, s], WS).then_inc(w_lo, 1)
                    for h in range(HALVES):
                        last = v.bn_stats(stats1[:, h, bass.ds(n * UNROLL + i, 1), :].rearrange("p a s -> p (a s)"),
                                          z[:, h, bass.ds(n * (UNROLL * CH) + i * CH, CH)])
                    last.then_inc(z_st, 1)

            with dve.Fori(0, CHUNKS // UNROLL) as n:
                turn_a(n)

            def batchnorm(stats_done, stats, mv, bn, vec, d, p):
                b, gamma, beta = vec
                dve.wait_ge(stats_done, CHUNKS)
                for h, st in enumerate(stats):
                    last = v.bn_aggr(mv[:, h, :], st)
                last.then_inc(d, 1)
                dve.wait_ge(d, 1)
                v.tensor_scalar(bn[:, 0, :], mv[:, :, 1], EPS, None, ALU.add).then_inc(d, 1)
                v.tensor_tensor(bn[:, 3, :], mv[:, :, 0], b, ALU.add).then_inc(d, 1)
                dve.wait_ge(p, 1)
                v.tensor_tensor(bn[:, 2, :], bn[:, 1, :], gamma, ALU.mult).then_inc(d, 1)
                dve.wait_ge(d, 4)
                v.tensor_tensor(bn[:, 0, :], b, bn[:, 3, :], ALU.subtract).then_inc(d, 1)
                dve.wait_ge(d, 5)
                v.tensor_tensor(bn[:, 1, :], bn[:, 0, :], bn[:, 2, :], ALU.mult).then_inc(d, 1)
                dve.wait_ge(d, 6)
                v.tensor_tensor(bn[:, 3, :], bn[:, 1, :], beta, ALU.add).then_inc(d, 1)

            dve.wait_ge(ld_misc, 144)
            batchnorm(z_st, [stats1[:, h, :, :].rearrange("p k s -> p (k s)") for h in range(HALVES)], mv1, bn1,
                      (v1[:, 0, :], v1[:, 1, :], v1[:, 2, :]), bn1_d, bn1_p)

            with dve.Fori(0, CHUNKS // UNROLL) as n:
                for i in range(UNROLL):
                    dve.wait_ge(o_mm, n * UNROLL + (i + 1))
                    v.tensor_scalar(z[:, 0, bass.ds(n * (UNROLL * CH) + i * CH, CH)], ps[:, i, :], 1.0, None, ALU.mult)
                    v.bn_stats(stats2[:, bass.ds(n * UNROLL + i, 1), :].rearrange("p a s -> p (a s)"),
                               ps[:, i, :]).then_inc(o_cp, 1)

            batchnorm(o_cp, [stats2[:, :, :].rearrange("p k s -> p (k s)")], mv2, bn2,
                      (v2[:, 0:1], v2[:, 1:2], v2[:, 2:3]), bn2_d, bn2_p)
            v.memset(mark[:, GCH:GCH + 1], 0.0).then_inc(y2_d, GCH)
            v.memset(mark[:, GCH + 1:GCH + 2], 0.0).then_inc(o_d, GCH)

            def lstm(g, u):
                t = u.thread
                c = cell[t][:, u.c % 2, 0:u.n]
                dve.wait_ge(g_a[t], gate_count(g, u, "g"))
                if u.s == 1:
                    v.tensor_tensor(c, gate_buf(u, "i"), gate_buf(u, "g"), ALU.mult).then_inc(c_d[t], 1)
                else:
                    v.tensor_tensor(gate_buf(u, "g"), gate_buf(u, "i"), gate_buf(u, "g"), ALU.mult).then_inc(ig_d[t], 1)
                    dve.wait_ge(ig_d[t], f_no(g, u))
                    dve.wait_ge(fc_p[t], f_no(g, u))
                    v.tensor_tensor(c, gate_buf(u, "g"), gate_buf(u, "f"), ALU.add).then_inc(c_d[t], 1)
                dve.wait_ge(tc_a[t], unit_no(g, u))
                v.scalar_tensor_tensor(out=gate_buf(u, "g"), in0=gate_buf(u, "o"), scalar=HS, in1=gate_buf(u, "i"),
                                       op0=ALU.mult, op1=ALU.mult).then_inc(h_d[t], 1)
                dve.wait_ge(h_d[t], unit_no(g, u))
                v.tensor_copy(h_out(g, u, 0), folded(gate_buf(u, "g"), u)).then_inc(hi_d[t], 1)

            def norm_stats(t, g, y, j, y_s, y_done, st_s, mv_s):
                dve.wait_ge(y_s, y_done)
                for b in range(CB):
                    last = v.bn_stats(lst[t][:, j, b, :], y[:, b * P:(b + 1) * P])
                last.then_inc(st_s, 1)
                mean_e, m2_e, mean_o, m2_o = (lst[t][:, j, :, k] for k in (1, 2, 4, 5))
                mean, diff, m2, sq, ve = (lmv[t][:, j, k, :] for k in range(5))
                dve.wait_ge(st_s, chunk_no(g, j))
                v.tensor_tensor(diff, mean_e, mean_o, ALU.subtract)
                v.scalar_tensor_tensor(out=m2, in0=m2_e, scalar=P * EPS, in1=m2_o, op0=ALU.add,
                                       op1=ALU.add).then_inc(mv_s, 1)
                dve.wait_ge(mv_s, g * (3 * GCH) + (3 * j + 1))
                v.scalar_tensor_tensor(out=mean, in0=diff, scalar=-0.5, in1=mean_e, op0=ALU.mult, op1=ALU.add)
                v.scalar_tensor_tensor(out=sq, in0=diff, scalar=0.25, in1=diff, op0=ALU.mult,
                                       op1=ALU.mult).then_inc(mv_s, 1)
                dve.wait_ge(mv_s, g * (3 * GCH) + (3 * j + 2))
                v.scalar_tensor_tensor(out=ve, in0=m2, scalar=1.0 / P, in1=sq, op0=ALU.mult,
                                       op1=ALU.add).then_inc(mv_s, 1)

            def norm_apply(t, g, y, o, j, rs_s, o_s):
                dve.wait_ge(rs_s, chunk_no(g, j))
                for b in range(CB):
                    at = slice(b * P, (b + 1) * P)
                    last = v.tensor_scalar(o[:, at], y[:, at], lmv[t][:, j, 0, b:b + 1], lrs[t][:, j, b:b + 1],
                                           ALU.subtract, ALU.mult)
                last.then_inc(o_s, 1)

            def conv_low(g, j, high_s, o_s, o, scalar, op):
                dve.wait_ge(high_s, chunk_no(g, j))
                v.scalar_tensor_tensor(out=o[:, 1, cols(j)], in0=ps[:, j, :], scalar=scalar, in1=o[:, 0, cols(j)],
                                       op0=op, op1=ALU.subtract).then_inc(o_s, 1)

            def turn_c(gx, gy):
                for item in ORDER:
                    g = gx if thread_of(item) == "x" else gy
                    if g is None:
                        continue
                    if isinstance(item, Unit):
                        lstm(g, item)
                        continue
                    kind, j = item
                    if kind == "norm1":
                        dve.wait_ge(tr_t, chunk_no(g, j))
                        dve.wait_ge(ld_xin[j], g * 16 + 16)
                        y = xin[:, j, :]
                        v.tensor_tensor(y, ps[:, j, :], y, ALU.add).then_inc(y_d, 1)
                        norm_stats("x", g, y, j, y_d, chunk_no(g, j), st_d, mv_d)
                    elif kind == "pair":
                        if not isinstance(g, int):
                            dve.wait_ge(stored[j], g * 16)
                        norm_apply("x", g, xin[:, j, :], x1[:, g % 2, cols(j)], j, rs_p, x1_d)
                    elif kind == "agg1":
                        conv_low(g, j, vh_a, vl_d, opB, 1.0 / WS, ALU.mult)
                    elif kind == "lin1":
                        conv_low(g, j, rh_a, rl_d, opA, 0.0, ALU.max)
                    elif kind == "lin2":
                        conv_low(g, j, sh_a, sl_d, opB, 1.0 / (WS * WS), ALU.mult)
                    elif kind == "agg2":
                        conv_low(g, j, h0h_a, h0l_d, opA, 0.0, ALU.max)
                    elif kind == "norm2":
                        dve.wait_ge(fin_t, chunk_no(g, j))
                        y = yT[:, j, :]
                        v.tensor_tensor(y, ps[:, bank0["y"] + j, :], x1[:, g % 2, cols(j)], ALU.add).then_inc(y2_d, 1)
                        norm_stats("y", g, y, j, y2_d, g * GCH + (GCH + j + 1), st2_d, mv2_d)
                    elif kind == "store":
                        norm_apply("y", g, yT[:, j, :], x1[:, g % 2, cols(j)], j, rs2_p, o_d)

            turns(dve, turn_c)

        @block.gpsimd
        def _(pool):
            gp = nc.gpsimd
            gp.memset(minus_half[:], -0.5).then_inc(pre_p, 1)
            gp.memset(zero, 0.0)
            for j in range(GCH):
                gp.memset(mark[:, j:j + 1], 0.0).then_inc(stored[j], 16)
            gp.memset(ones, 1.0).then_inc(pre_p, 1)
            pool.wait_ge(pre_p, 2)
            pool.wait_ge(pre_d, 5)
            gp.tensor_tensor(sm[:, 5:6], sm[:, 4:5], minus_half[:, 0:1], ALU.pow).then_inc(pre_p, 1)
            for bn, h, d, p in ((bn1, HALVES, bn1_d, bn1_p), (bn2, 1, bn2_d, bn2_p)):
                pool.wait_ge(d, 2)
                gp.tensor_tensor(bn[:, 1, :], bn[:, 0, :], minus_half[:, 0:h], ALU.pow).then_inc(p, 1)

            def lstm(g, u):
                t = u.thread
                if u.s > 1:
                    pool.wait_ge(g_a[t], gate_count(g, u, "f"))
                    gp.tensor_tensor(gate_buf(u, "f"), gate_buf(u, "f"), cell[t][:, u.c % 2, 0:u.n],
                                     ALU.mult).then_inc(fc_p[t], 1)
                pool.wait_ge(hi_d[t], unit_no(g, u))
                gp.tensor_tensor(h_out(g, u, 1), folded(gate_buf(u, "g"), u), h_out(g, u, 0),
                                 ALU.subtract).then_inc(lo_p[t], 1)

            def rstd(t, g, j, mv_s, rs_s):
                pool.wait_ge(mv_s, g * (3 * GCH) + 3 * (j + 1))
                gp.tensor_tensor(lrs[t][:, j, :], lmv[t][:, j, 4, :], minus_half[:], ALU.pow).then_inc(rs_s, 1)

            def turn_c(gx, gy):
                for item in ORDER:
                    g = gx if thread_of(item) == "x" else gy
                    if g is None:
                        continue
                    if isinstance(item, Unit):
                        lstm(g, item)
                        continue
                    kind, j = item
                    if kind == "norm1":
                        rstd("x", g, j, mv_d, rs_p)
                    elif kind == "pair":
                        pool.wait_ge(x1h_a, chunk_no(g, j))
                        gp.tensor_tensor(opA[:, 1, cols(j)], x1[:, g % 2, cols(j)], opA[:, 0, cols(j)],
                                         ALU.subtract).then_inc(x1l_p, 1)
                    elif kind == "norm2":
                        rstd("y", g, j, mv2_d, rs2_p)

            turns(pool, turn_c)


def kernel(**inputs):
    import numpy as _np
    import concourse.bacc as _bacc
    from concourse import mybir as _mybir
    from concourse.bass_utils import run_bass_kernel_spmd as _run

    a = {k: _np.asarray(v) for k, v in inputs.items()}

    def column(v, n):
        return v.reshape(n, P).T

    consts = _np.zeros((P, P + 8), _np.float32)
    consts[:, :P] = _np.eye(P)
    for c, rows in enumerate(((0, 2), (1, 3), (0, 1), (2, 3), (0,), (1,), (0, 1))):
        consts[list(rows), P + c] = 1.0

    host = {
        "xn": a["x"].transpose(1, 0, 2).reshape(P, COLS),
        "adj": a["adj"],
        "adjT": a["adj"].T,
        "W1T": a["L0_gnn_W1"].T,
        "W2T": a["L0_gnn_W2"].T.reshape(HALVES, P, P).transpose(1, 0, 2),
        "vec1": _np.stack([column(a[f"L0_gnn_{n}"], HALVES) for n in ("b1", "g1", "be1")], 1),
        "vec2": _np.stack([a[f"L0_gnn_{n}"] for n in ("b2", "g2", "be2")], 1),
        "Wg0": a["L1_gnn_Wg0"],
        "Wg1": a["L1_gnn_Wg1"],
        "bg0": _np.broadcast_to(a["L1_gnn_bg0"], (P, P)),
        "bg1": _np.broadcast_to(a["L1_gnn_bg1"], (P, P)),
        "WihT": a["L1_gnn_Wih"].transpose(2, 0, 1).reshape(P, -1),
        "WhhT": a["L1_gnn_Whh"].transpose(2, 0, 1).reshape(P, -1),
        "bih": column(a["L1_gnn_bih"].reshape(-1), MAX_SKIP * 4),
        "bhh": column(a["L1_gnn_bhh"].reshape(-1), MAX_SKIP * 4),
        "consts": consts,
    }
    nc = _bacc.Bacc("TRN2", target_bir_lowering=False, num_devices=1)
    arrays, args = {}, []
    for name, v in host.items():
        v = _np.ascontiguousarray(v)
        arrays[f"in_{name}_dram"] = v
        args.append(nc.dram_tensor(f"in_{name}_dram", v.shape, _mybir.dt.from_np(v.dtype), kind="ExternalInput").ap())
    args.append(nc.dram_tensor("out_dram", (P, COLS), F32, kind="ExternalOutput").ap())
    gnn_kernel(nc, *args)
    r = _run(nc, [arrays], core_ids=[0])
    got = r.results[0]["out_dram"]
    return _np.ascontiguousarray(got.reshape(P, B, P).transpose(1, 0, 2))
```

```python
from collections import namedtuple
from contextlib import ExitStack

import concourse.bass as bass
from concourse import mybir

F32 = mybir.dt.float32
F16 = mybir.dt.float16
ALU = mybir.AluOpType
ACT = mybir.ActivationFunctionType

P = 128
B = 128
HID = 256
HALVES = HID // P
COLS = B * P
CB = 4
CH = CB * P
CHUNKS = B // CB
UNROLL = 4
GB = 16
GC = GB * P
GCH = GB // CB
GROUPS = B // GB
EPS = 1e-5

WS = 64.0
HS = 256.0
MAX_SKIP = 4
WSL = MAX_SKIP * 4 * P // CHUNKS
GATE = {"i": 0, "f": 1, "g": 2, "o": 3}
BANK = {"i": 0, "g": 1, "f": 2, "o": 3}

BANK_GATE = "igfo"

Unit = namedtuple("Unit", "thread p s c b0 nb nw n k gate0")


def lstm_units(thread, plan):
    units, gate0 = [], 0
    for k, (p, s, c, b0, nb) in enumerate(plan):
        nw = P // p
        units.append(Unit(thread, p, s, c, b0, nb, nw, nb * nw, k, gate0))
        gate0 += 3 if s == 1 else 4
    return units, gate0


X_UNITS, X_GATES = lstm_units("x", [(1, 1, j, CB * j, CB) for j in range(GCH)]
                              + [(2, 1, c, 8 * c, 8) for c in range(2)]
                              + [(2, 2, c, 8 * c, 8) for c in range(2)])
Y_UNITS, Y_GATES = lstm_units("y", [(3, s, c, 8 * c, 8) for s in (1, 2, 3) for c in range(2)]
                              + [(4, s, 0, 0, GB) for s in (1, 2, 3, 4)])
NX, NY = len(X_UNITS), len(Y_UNITS)


def unit(p, s, c=0):
    return next(u for u in X_UNITS + Y_UNITS if (u.p, u.s, u.c) == (p, s, c))


def gates(u):
    return "igo" if u.s == 1 else "figo"


def gate_no(u, q):
    return u.gate0 + gates(u).index(q) + 1


PE_ORDER = """
    agg1.0 agg1.1 agg1.2 input.310 agg1.3 input.311 input.320 lin1.0 lin1.1 lin1.2 hidden.320 norm1.0
    input.321 hidden.321 lin2.0 input.330 hidden.330 norm1.1 input.331 hidden.331 lin1.3 norm1.2 agg2.0
    lin2.1 lin2.2 norm1.3 input.410 agg2.1 agg2.2 lin2.3 input.420 agg2.3 hidden.420 input.110 input.430
    input.111 hidden.430 input.112 input.113 input.440 hidden.440 input.210 input.211 input.220 norm2.0
    norm2.1 norm2.2 norm2.3 hidden.220 input.221 hidden.221"""
ACT_ORDER = """
    agg1.0 agg1.1 gates.310.igo agg1.2 yT.0 yT.1 agg1.3 gates.311.igo tanh.310 tanh.311 lin1.0 lin1.1 lin1.2
    gates.320.figo yT.2 tanh.320 gates.321.figo lin2.0 tanh.321 apply1.0 applied.0 gates.330.figo yT.3
    tanh.330 gates.331.figo lin1.3 tanh.331 agg2.0 apply1.1 lin2.1 lin2.2 applied.1 gates.410.igo agg2.1
    agg2.2 tanh.410 lin2.3 apply1.2 agg2.3 applied.2 gates.420.figo gates.110.ig tanh.420 gates.110.o x1.0
    tanh.110 apply1.3 applied.3 gates.111.igo gates.430.fig tanh.111 gates.112.igo gates.430.o tanh.430
    tanh.112 x1.1 gates.113.igo x1.2 gates.440.f tanh.113 gates.440.igo gates.210.igo tanh.440 gates.211.igo
    tanh.210 x1.3 tanh.211 gates.220.figo tanh.220 gates.221.figo tanh.221"""
DVE_ORDER = """
    agg1.0 agg1.1 h.310 agg1.2 lin1.0 h.311 lin1.1 agg1.3 lin1.2 ig.320 sum1.0 cell.320 stats1.0 h.320
    ig.321 cell.321 lin2.0 h.321 sum1.1 ig.330 cell.330 stats1.1 h.330 ig.331 cell.331 sum1.2 h.331 lin1.3
    agg2.0 sum1.3 lin2.1 lin2.2 stats1.2 agg2.1 agg2.2 h.410 lin2.3 stats1.3 agg2.3 ig.420 cell.420 h.420
    h.110 ig.430 cell.430 h.111 h.430 h.112 h.113 ig.440 cell.440 h.440 h.210 sum2.0 stats2.0 h.211 sum2.1
    stats2.1 ig.220 store.0 cell.220 store.1 h.220 sum2.2 ig.221 cell.221 sum2.3 stats2.2 h.221 stats2.3
    store.2 store.3"""
POOL_ORDER = """
    c1.310 c1.311 h.310 h.311 fc.320 fc.321 rstd1.0 h.320 h.321 fc.330 fc.331 rstd1.1 h.330 h.331 c1.410
    rstd1.2 h.410 rstd1.3 fc.420 c1.110 h.420 x1.0 h.110 c1.111 fc.430 c1.112 h.111 h.430 c1.113 h.112
    fc.440 h.113 x1.1 c1.210 x1.2 h.440 c1.211 h.210 x1.3 rstd2.0 h.211 fc.220 rstd2.1 fc.221 h.220 rstd2.2
    h.221 rstd2.3"""
THREAD = {"yT": "w", "norm1": "w", "sum1": "w", "stats1": "w", "rstd1": "w", "apply1": "w", "applied": "w", "x1": "w",
          "norm2": "y", "sum2": "y", "stats2": "y", "rstd2": "y", "store": "y"}


def steps(order, groups):
    for step in order.split():
        kind, where, *some = step.split(".")
        if len(where) > 1:
            item = unit(*(int(c) for c in where))
            thread = item.thread
        else:
            item, thread = int(where), THREAD.get(kind, "x")
        if groups[thread] is not None:
            yield kind, item, some[0] if some else "", groups[thread]


def gnn_kernel(nc, xn, adj, adjT, W1T, W2T, vec1, vec2, Wg0, Wg1, bg0, bg1, WihT, WhhT, bih, bhh,
               consts, out):
    ctx = ExitStack()
    with ctx:
        def sb(name, shape, dt=F32):
            return ctx.enter_context(nc.sbuf_tensor(name, shape, dt))

        def sem(name):
            return ctx.enter_context(nc.semaphore(name))

        z = sb("z", [P, HALVES, COLS])
        late = z[:, 1, :]

        def carve(at, n, dt=F32):
            return late[:, at:at + n] if dt is F32 else late[:, at:at + n].bitcast(dt)

        x1 = carve(0, 3 * GC).rearrange("p (t c) -> p t c", t=3)
        opA = carve(6144, GC, F16).rearrange("p (l c) -> p l c", l=2)
        opB = carve(8192, GC, F16).rearrange("p (l c) -> p l c", l=2)
        H = carve(10240, 2 * GC, F16).rearrange("p (t l c) -> p t l c", t=2, l=2)
        xin = carve(14336, GCH * CH).rearrange("p (j c) -> p j c", j=GCH)

        gbuf = {t: sb(f"gbuf_{t}", [P, 2, 4, CH]) for t in "xy"}
        cell = {t: sb(f"cell_{t}", [P, 2, CH]) for t in "xy"}
        hst = {t: sb(f"hst_{t}", [P, 2, 2, CH], F16) for t in "xy"}
        wst = gbuf["x"][:, :, :, :].rearrange("p a q c -> p (a q c)").rearrange("p (m c) -> p m c", m=2)
        W = sb("W", [P, 2, 2, MAX_SKIP * 4 * P], F16)
        xa = gbuf["y"][:, :, :, :].rearrange("p a q c -> p (a q) c")
        x_ring, agg = xa[:, 0:4, :], xa[:, 4:6, :]
        early = cell["x"][:, :, :].rearrange("p a (q c) -> p (a q) c", c=P)
        tmp, ones, zero = early[:, 0:4, :], early[:, 4, :], early[:, 5, :]
        early = cell["y"][:, :, :].rearrange("p a (q c) -> p (a q) c", c=P)
        adj_n, adj_t, wg, bgr = early[:, 0, :], early[:, 1, :], early[:, 2:4, :], early[:, 4:6, :]
        ahat = early[:, 6, :]
        early = hst["x"][:, :, :, :].rearrange("p a l c -> p (a l c)").bitcast(F32)
        w1, w2 = early[:, 0:HID], early[:, HID:2 * HID].rearrange("p (h c) -> p h c", h=HALVES)
        v1 = sb("v1", [P, 3, HALVES])
        v2 = sb("v2", [P, 3])
        cst = sb("cst", [P, P + 8])
        ident = cst[:, 0:P]
        bi = sb("bi", [P, 2, MAX_SKIP * 4])
        gbias = sb("gbias", [P, MAX_SKIP * 4])
        adjh = sb("adjh", [P, 2, P], F16)
        wgh = sb("wgh", [P, 2, 2, P], F16)
        idh = sb("idh", [P, P], F16)
        bias1_w = sb("bias1_w", [P, P], F16)
        bias1_x = sb("bias1_x", [P, CB, P], F16)
        bias2_w = sb("bias2_w", [P, P], F16)
        bias2_x = sb("bias2_x", [P, CB, P], F16)
        tmph = sb("tmph", [P, 2, P], F16)
        minus_half = sb("minus_half", [P, CB])
        sm = sb("sm", [P, 6])
        mark = sb("mark", [P, GCH + 1])
        early = hst["y"][:, :, :, :].rearrange("p a l c -> p (a l c)").bitcast(F32)
        stats1 = early[:, 0:HALVES * CHUNKS * 6].rearrange("p (h k s) -> p h k s", h=HALVES, k=CHUNKS)
        stats2 = stats1[:, 0, :, :]
        mv1 = sb("mv1", [P, HALVES, 2])
        mv2 = sb("mv2", [P, 1, 2])
        bn1 = sb("bn1", [P, 4, HALVES])
        bn2 = sb("bn2", [P, 4, 1])
        lst = {t: sb(f"lst_{t}", [P, GCH, CB, 6]) for t in "xy"}
        lmv = {t: sb(f"lmv_{t}", [P, GCH, 5, CB]) for t in "xy"}
        lrs = {t: sb(f"lrs_{t}", [P, GCH, CB]) for t in "xy"}
        nmr = sb("nmr", [P, GCH, CB])
        yT = sb("yT", [P, 2, CH])
        y2 = sb("y2", [P, 2, CH])

        ps = ctx.enter_context(nc.psum_tensor("ps", [P, 8, CH], F32))
        bank0 = {"x": 0, "y": 4}

        ld_adj, ld_w1, ld_misc, ld_lstm = sem("ld_adj"), sem("ld_w1"), sem("ld_misc"), sem("ld_lstm")
        ld_x = [sem(f"ld_x{i}") for i in range(UNROLL)]
        ld_xin = [sem(f"ld_xin{i}") for i in range(GCH)]
        pre_d, pre_a, pre_p, pre_t = sem("pre_d"), sem("pre_a"), sem("pre_p"), sem("pre_t")
        w_hi, w_lo = sem("w_hi"), sem("w_lo")
        agg_mm, agg_cp = sem("agg_mm"), sem("agg_cp")
        z_mm, z_cp, z_st = sem("z_mm"), sem("z_cp"), sem("z_st")
        bn1_d, bn1_p = sem("bn1_d"), sem("bn1_p")
        r_act, o_mm, o_cp, o_st = sem("r_act"), sem("o_mm"), sem("o_cp"), sem("o_st")
        bn2_d, bn2_p = sem("bn2_d"), sem("bn2_p")
        yT_a, tr_t, y_d, st_d, mv_d, rs_p, x1_a, x1h_a, x1l_p = (
            sem(n) for n in ("yT_a", "tr_t", "y_d", "st_d", "mv_d", "rs_p", "x1_a", "x1h_a", "x1l_p"))
        agg1_t, lin1_t, lin2_t, agg2_t = (sem(n) for n in ("agg1_t", "lin1_t", "lin2_t", "agg2_t"))
        vh_a, rh_a, sh_a, h0h_a = (sem(n) for n in ("vh_a", "rh_a", "sh_a", "h0h_a"))
        vl_d, rl_d, sl_d, h0l_d = (sem(n) for n in ("vl_d", "rl_d", "sl_d", "h0l_d"))
        fin_t, y2_d, st2_d, mv2_d, rs2_p, o_d = (
            sem(n) for n in ("fin_t", "y2_d", "st2_d", "mv2_d", "rs2_p", "o_d"))
        stored = [sem(f"stored{j}") for j in range(GCH)]
        g_t = {t: sem(f"g_t_{t}") for t in "xy"}
        g_a = {t: sem(f"g_a_{t}") for t in "xy"}
        ig_d = {t: sem(f"ig_d_{t}") for t in "xy"}
        fc_p = {t: sem(f"fc_p_{t}") for t in "xy"}
        c1_p = {t: sem(f"c1_p_{t}") for t in "xy"}
        c_d = {t: sem(f"c_d_{t}") for t in "xy"}
        tc_a = {t: sem(f"tc_a_{t}") for t in "xy"}
        h_d = {t: sem(f"h_d_{t}") for t in "xy"}
        hi_d = {t: sem(f"hi_d_{t}") for t in "xy"}
        lo_p = {t: sem(f"lo_p_{t}") for t in "xy"}

        UNITS = {"x": NX, "y": NY}
        NGATES = {"x": X_GATES, "y": Y_GATES}

        def chunk_no(g, j):
            return g * GCH + (j + 1)

        def unit_no(g, u):
            return g * UNITS[u.thread] + (u.k + 1)

        def gate_count(g, u, q):
            return g * NGATES[u.thread] + gate_no(u, q)

        def step_no(g, u, first):
            units = X_UNITS if u.thread == "x" else Y_UNITS
            return g * sum((w.s == 1) == first for w in units) + sum((w.s == 1) == first for w in units[:u.k + 1])

        def first_no(g, u):
            return step_no(g, u, True)

        def f_no(g, u):
            return step_no(g, u, False)

        def before(u):
            return (X_UNITS if u.thread == "x" else Y_UNITS)[u.k - 1]

        def cols(j):
            return slice(j * CH, (j + 1) * CH)

        def windows(hp, u, t):
            v = hp.rearrange("p (b t) -> p b t", t=P)
            return v[:, u.b0:u.b0 + u.nb, t:t + u.p * (u.nw - 1) + 1:u.p]

        def folded(ap, u):
            return ap.rearrange("p (b w) -> p b w", w=u.nw)

        def gate_buf(u, q):
            return gbuf[u.thread][:, u.k % 2, BANK[q], 0:u.n]

        def h_out(g, u, part):
            if u.s == u.p:
                return windows(H[:, g % 2, part, :], u, u.p - 1)
            return folded(hst[u.thread][:, u.c, part, 0:u.n], u)

        block = ctx.enter_context(nc.Block())

        def turns(eng, body):
            body(0, None, None)
            body(1, 0, None)
            with eng.Fori(1, GROUPS - 1) as g:
                body(g + 1, g, g - 1)
            body(None, GROUPS - 1, GROUPS - 2)
            body(None, None, GROUPS - 1)

        @block.sync
        def _(sp):
            for dst, src in ((adj_n, adj), (adj_t, adjT), (cst[:], consts)):
                sp.dma_start(dst, src).then_inc(ld_adj, 16)
            sp.dma_start(w1, W1T).then_inc(ld_w1, 16)
            for i in range(UNROLL):
                sp.dma_start(x_ring[:, i, :], xn[:, cols(i)]).then_inc(ld_x[i], 16)
            for dst, src in ((v1[:], vec1), (v2[:], vec2), (w2, W2T), (wg[:, 0, :], Wg0), (wg[:, 1, :], Wg1),
                             (bgr[:, 0, :], bg0), (bgr[:, 1, :], bg1), (bi[:, 0, :], bih), (bi[:, 1, :], bhh)):
                sp.dma_start(dst, src).then_inc(ld_misc, 16)
            sp.dma_start(wst[:, 0, :], WihT).then_inc(ld_lstm, 16)
            sp.dma_start(wst[:, 1, :], WhhT).then_inc(ld_lstm, 16)
            with sp.Fori(1, CHUNKS // UNROLL) as n:
                for i in range(UNROLL):
                    sp.wait_ge(agg_mm, (n - 1) * UNROLL + (i + 1))
                    sp.dma_start(x_ring[:, i, :], xn[:, bass.ds(n * (UNROLL * CH) + i * CH, CH)]).then_inc(ld_x[i], 16)

            sp.wait_ge(o_mm, CHUNKS)
            for j in range(GCH):
                sp.dma_start(xin[:, j, :], xn[:, cols(j)]).then_inc(ld_xin[j], 16)

            def turn_c(gw, gx, gy):
                if gw is not None and not (isinstance(gw, int) and gw == 0):
                    for j in range(GCH):
                        sp.wait_ge(x1_a, gw * GCH - (GCH - 1) + j)
                        sp.dma_start(xin[:, j, :], xn[:, bass.ds(gw * GC + j * CH, CH)]).then_inc(ld_xin[j], 16)
                if gy is not None:
                    for j in range(GCH):
                        sp.wait_ge(o_d, chunk_no(gy, j))
                        sp.dma_start(out[:, bass.ds(gy * GC + j * CH, CH)], x1[:, gy % 3, cols(j)]).then_inc(stored[j], 16)

            turns(sp, turn_c)
            for j in range(GCH):
                sp.wait_ge(stored[j], 16 * (GROUPS + 1))

        @block.tensor
        def _(pe):
            def mm(o, w, m, start, stop):
                return pe.matmul(o, w, m, start=start, stop=stop, skip_group_check=True)

            pe.wait_ge(ld_adj, 48)
            pe.wait_ge(pre_p, 2)
            mm(ps[:, 1, 0:P], ones, adj_t, True, True).then_inc(pre_t, 1)
            pe.wait_ge(pre_d, 6)
            pe.transpose(ps[:, 0, 0:P], tmp[:, 1, :], ident).then_inc(pre_t, 1)
            pe.wait_ge(pre_d, 8)
            pe.wait_ge(ld_w1, 16)

            def aggregate(n, i):
                k = n * UNROLL + i
                pe.wait_ge(ld_x[i], n * 16 + 16)
                if not (isinstance(k, int) and k < 2):
                    pe.wait_ge(agg_cp, k - 1)
                for b in range(CB):
                    last = mm(ps[:, i % 2, b * P:(b + 1) * P], x_ring[:, i, b * P:(b + 1) * P], ahat, True, True)
                last.then_inc(agg_mm, 1)

            def hidden(n, i):
                k = n * UNROLL + i
                pe.wait_ge(agg_cp, k + 1)
                if not (isinstance(k, int) and k < 2):
                    pe.wait_ge(z_cp, k - 1)
                for h in range(HALVES):
                    last = mm(ps[:, 2 + 2 * (i % 2) + h, :], w1[:, h * P:(h + 1) * P], agg[:, i % 2, :], True, True)
                last.then_inc(z_mm, 1)

            def turn_a(n):
                aggregate(n, 0)
                for i in range(1, UNROLL):
                    aggregate(n, i)
                    hidden(n, i - 1)
                hidden(n, UNROLL - 1)

            turn_a(0)
            with pe.Fori(1, CHUNKS // UNROLL) as n:
                turn_a(n)

            def turn_b(n):
                for i in range(UNROLL):
                    k = n * UNROLL + i
                    if not isinstance(n, int):
                        pe.wait_ge(o_cp, k - (UNROLL - 1))
                    pe.wait_ge(r_act, k + 1)
                    for h in range(HALVES):
                        last = mm(ps[:, i, :], w2[:, h, :], z[:, h, bass.ds(n * (UNROLL * CH) + i * CH, CH)],
                                  h == 0, h == HALVES - 1)
                    last.then_inc(o_mm, 1)

            pe.wait_ge(ld_misc, 144)
            pe.wait_ge(z_cp, CHUNKS)
            turn_b(0)
            with pe.Fori(1, CHUNKS // UNROLL) as n:
                turn_b(n)

            pe.wait_ge(o_cp, CHUNKS)
            pe.wait_ge(w_lo, CHUNKS)

            def node_products(o, stat, mov, j, first):
                for b in range(CB):
                    at = slice(j * CH + b * P, j * CH + (b + 1) * P)
                    mm(o[:, b * P:(b + 1) * P], stat[:, 0, at], mov[:, 0, :], first, False)
                    mm(o[:, b * P:(b + 1) * P], stat[:, 0, at], mov[:, 1, :], False, False)
                    last = mm(o[:, b * P:(b + 1) * P], stat[:, 1, at], mov[:, 0, :], False, True)
                return last

            def input_products(g, u):
                t, bank, prev = u.thread, bank0[u.thread], before(u)
                if u == unit(1, 1, 0):
                    pe.wait_ge(h0l_d, chunk_no(g, GCH - 1))
                elif u.p == 1:
                    pe.wait_ge(h0l_d, chunk_no(g, u.c))
                elif u.p == 2 and u.s == 1:
                    pe.wait_ge(lo_p["x"], unit_no(g, unit(1, 1, 2 * u.c + 1)))
                elif u.p == 3 and u.s == 1:
                    pe.wait_ge(lo_p["x"], unit_no(g, unit(2, 2, u.c)))
                    if u.c == 0:
                        pe.wait_ge(y2_d, g * GCH + GCH)
                elif u.p == 4 and u.s == 1:
                    pe.wait_ge(lo_p["y"], unit_no(g, unit(3, 3, 1)))
                src = opA if u.p == 1 else H[:, g % 2, :, :]
                for q in gates(u):
                    if u.k and q in gates(prev):
                        pe.wait_ge(g_a[t], gate_count(g, prev, q))
                    o = ps[:, bank + BANK[q], 0:u.n]
                    at = (u.p - 1) * 4 * P + GATE[q] * P
                    w = [W[:, 0, part, at:at + P] for part in range(2)]
                    x = [windows(src[:, part, :], u, u.s - 1) for part in range(2)]
                    mm(o, w[0], x[0], True, False)
                    mm(o, w[1], x[0], False, False)
                    last = mm(o, w[0], x[1], False, u.s == 1)
                    if u.s == 1:
                        last.then_inc(g_t[t], 1)

            def hidden_products(g, u):
                t, bank = u.thread, bank0[u.thread]
                pe.wait_ge(hi_d[t], unit_no(g, unit(u.p, u.s - 1, u.c)))
                for n, q in enumerate(gates(u)):
                    o = ps[:, bank + BANK[q], 0:u.n]
                    at = (u.p - 1) * 4 * P + GATE[q] * P
                    w = [W[:, 1, part, at:at + P] for part in range(2)]
                    h = [hst[t][:, u.c, part, 0:u.n] for part in range(2)]
                    mm(o, w[0], h[0], False, False)
                    mm(o, w[1], h[0], False, False)
                    if n == 0:
                        pe.wait_ge(lo_p[t], unit_no(g, unit(u.p, u.s - 1, u.c)))
                    mm(o, w[0], h[1], False, True).then_inc(g_t[t], 1)

            def turn_c(gw, gx, gy):
                for kind, j, _, g in steps(PE_ORDER, {"w": gw, "x": gx, "y": gy}):
                    if kind == "input":
                        input_products(g, j)
                        continue
                    if kind == "hidden":
                        hidden_products(g, j)
                        continue
                    o = ps[:, j, :]
                    if kind == "norm1":
                        if gx is not None:
                            pe.wait_ge(rl_d, chunk_no(gx, j))
                        pe.wait_ge(yT_a, chunk_no(g, j))
                        for b in range(CB):
                            last = pe.transpose(o[:, b * P:(b + 1) * P], yT[:, j % 2, b * P:(b + 1) * P], ident)
                        last.then_inc(tr_t, 1)
                    elif kind == "agg1":
                        if not (isinstance(g, int) and g == 0):
                            pe.wait_ge(g_a["x"], gate_count(g - 1, unit(2, 2, 1), BANK_GATE[j]))
                        pe.wait_ge(x1h_a, chunk_no(g, j))
                        pe.wait_ge(x1l_p, chunk_no(g, j))
                        node_products(o, opA, adjh, j, True).then_inc(agg1_t, 1)
                    elif kind == "lin1":
                        pe.wait_ge(vl_d, chunk_no(g, j))
                        mm(o, bias1_w[:], bias1_x[:, :, :].rearrange("p b c -> p (b c)"), True, False)
                        mm(o, wgh[:, 0, 0, :], opB[:, 0, cols(j)], False, False)
                        mm(o, wgh[:, 0, 1, :], opB[:, 0, cols(j)], False, False)
                        mm(o, wgh[:, 0, 0, :], opB[:, 1, cols(j)], False, True).then_inc(lin1_t, 1)
                    elif kind == "lin2":
                        pe.wait_ge(rl_d, chunk_no(g, j))
                        if gw is not None:
                            pe.wait_ge(y_d, chunk_no(gw, j))
                        mm(o, bias2_w[:], bias2_x[:, :, :].rearrange("p b c -> p (b c)"), True, False)
                        node_products(o, opA, wgh[:, 1, :, :], j, False).then_inc(lin2_t, 1)
                    elif kind == "agg2":
                        pe.wait_ge(sl_d, chunk_no(g, j))
                        node_products(o, opB, adjh, j, True).then_inc(agg2_t, 1)
                    elif kind == "norm2":
                        o = ps[:, bank0["y"] + j, :]
                        if j == 0:
                            pe.wait_ge(lo_p["y"], unit_no(g, unit(4, 4)))
                        for b in range(CB):
                            at = slice(j * CH + b * P, j * CH + (b + 1) * P)
                            mm(o[:, b * P:(b + 1) * P], H[:, g % 2, 0, at], idh[:], True, False)
                            last = mm(o[:, b * P:(b + 1) * P], H[:, g % 2, 1, at], idh[:], False, True)
                        last.then_inc(fin_t, 1)

            turns(pe, turn_c)

        @block.scalar
        def _(act):
            a = nc.scalar.activation

            act.wait_ge(ld_adj, 48)
            a(adjh[:, 0, :], adj_t, ACT.Copy, scale=WS).then_inc(pre_a, 1)
            act.wait_ge(ld_misc, 144)
            a(wgh[:, :, 0, :], wg, ACT.Copy, scale=WS).then_inc(pre_a, 1)
            a(idh[:], ident, ACT.Copy, scale=1.0 / HS).then_inc(pre_a, 1)

            def turn_a(n):
                for step in range(UNROLL + 1):
                    if step < UNROLL:
                        i = step
                        k = n * UNROLL + i
                        act.wait_ge(agg_mm, k + 1)
                        if not (isinstance(k, int) and k < 2):
                            act.wait_ge(z_mm, k - 1)
                        a(agg[:, i % 2, :], ps[:, i % 2, :], ACT.Copy).then_inc(agg_cp, 1)
                    if step:
                        i = step - 1
                        k = n * UNROLL + i
                        act.wait_ge(z_mm, k + 1)
                        a(z[:, :, bass.ds(n * (UNROLL * CH) + i * CH, CH)],
                          ps[:, 2 + 2 * (i % 2):4 + 2 * (i % 2), :], ACT.Copy).then_inc(z_cp, 1)
                        if isinstance(n, int) and step == 1:
                            act.wait_ge(ld_lstm, 32)
                        s = bass.ds(n * (UNROLL * WSL) + i * WSL, WSL)
                        a(W[:, :, 0, s], wst[:, :, s], ACT.Copy, scale=WS).then_inc(w_hi, 1)

            turn_a(0)
            with act.Fori(1, CHUNKS // UNROLL) as n:
                turn_a(n)

            act.wait_ge(bn1_d, 7)
            with act.Fori(0, CHUNKS // UNROLL) as n:
                for i in range(UNROLL):
                    for h in range(HALVES):
                        at = z[:, h, bass.ds(n * (UNROLL * CH) + i * CH, CH)]
                        last = a(at, at, ACT.Relu, bias=bn1[:, 3, h:h + 1], scale=bn1[:, 2, h:h + 1])
                    last.then_inc(r_act, 1)

            act.wait_ge(bn2_d, 7)

            def nonlinear(g, u, some):
                t = u.thread
                scale = 1.0 / (WS * (WS if u.p == 1 else HS))
                for q in some:
                    if u.k >= 2 and q == gates(u)[0]:
                        act.wait_ge(lo_p[t], g * UNITS[t] + (u.k - 1))
                    act.wait_ge(g_t[t], gate_count(g, u, q))
                    at = (u.p - 1) * 4 + GATE[q]
                    a(gate_buf(u, q), ps[:, bank0[t] + BANK[q], 0:u.n], ACT.Tanh if q == "g" else ACT.Sigmoid,
                      bias=gbias[:, at:at + 1], scale=scale).then_inc(g_a[t], 1)

            def turn_c(gw, gx, gy):
                for kind, j, some, g in steps(ACT_ORDER, {"w": gw, "x": gx, "y": gy}):
                    if kind == "gates":
                        nonlinear(g, j, some)
                    elif kind == "tanh":
                        t = j.thread
                        if j.s == 1:
                            act.wait_ge(c1_p[t], first_no(g, j))
                        else:
                            act.wait_ge(c_d[t], f_no(g, j))
                        a(gate_buf(j, "i"), cell[t][:, j.c % 2, 0:j.n], ACT.Tanh).then_inc(tc_a[t], 1)
                    elif kind == "yT":
                        if not (isinstance(g, int) and g == 0 and j < 2):
                            act.wait_ge(tr_t, g * GCH + (j - 1))
                        a(yT[:, j % 2, :], z[:, 0, bass.ds(g * GC + j * CH, CH)], ACT.Identity,
                          bias=bn2[:, 3, 0:1], scale=bn2[:, 2, 0:1]).then_inc(yT_a, 1)
                    elif kind == "apply1":
                        act.wait_ge(rs_p, g * (2 * GCH) + 2 * (j + 1))
                        if not (isinstance(g, int) and g < 3):
                            act.wait_ge(stored[j], g * 16 - 16)
                        for b in range(CB):
                            at = slice(b * P, (b + 1) * P)
                            last = a(x1[:, g % 3, j * CH + b * P:j * CH + (b + 1) * P], xin[:, j, at], ACT.Identity,
                                     bias=nmr[:, j, b:b + 1], scale=lrs["x"][:, j, b:b + 1])
                        last.then_inc(x1_a, 1)
                    elif kind == "applied":
                        act.wait_ge(x1_a, chunk_no(g, j))
                    elif kind == "x1":
                        a(opA[:, 0, cols(j)], x1[:, g % 3, cols(j)], ACT.Copy).then_inc(x1h_a, 1)
                    elif kind == "agg1":
                        act.wait_ge(agg1_t, chunk_no(g, j))
                        a(opB[:, 0, cols(j)], ps[:, j, :], ACT.Copy, scale=1.0 / WS).then_inc(vh_a, 1)
                    elif kind == "lin1":
                        act.wait_ge(lin1_t, chunk_no(g, j))
                        a(opA[:, 0, cols(j)], ps[:, j, :], ACT.Relu).then_inc(rh_a, 1)
                    elif kind == "lin2":
                        act.wait_ge(lin2_t, chunk_no(g, j))
                        a(opB[:, 0, cols(j)], ps[:, j, :], ACT.Copy, scale=1.0 / (WS * WS)).then_inc(sh_a, 1)
                    elif kind == "agg2":
                        act.wait_ge(agg2_t, chunk_no(g, j))
                        a(opA[:, 0, cols(j)], ps[:, j, :], ACT.Relu).then_inc(h0h_a, 1)

            turns(act, turn_c)

        @block.vector
        def _(dve):
            v = nc.vector

            dve.wait_ge(ld_adj, 48)
            v.tensor_tensor(tmp[:, 0, :], adj_n, ident, ALU.add).then_inc(pre_d, 1)
            v.tensor_tensor(tmp[:, 2, :], adj_t, ident, ALU.add).then_inc(pre_d, 1)
            dve.wait_ge(pre_d, 2)
            v.reduce_sum(sm[:, 0:1], tmp[:, 0, :], mybir.AxisListType.X)
            v.reduce_sum(sm[:, 1:2], tmp[:, 2, :], mybir.AxisListType.X)
            v.tensor_tensor(tmp[:, 3, :], tmp[:, 0, :], ident, ALU.mult).then_inc(pre_d, 1)
            dve.wait_ge(pre_d, 3)
            v.reduce_sum(sm[:, 2:3], tmp[:, 3, :], mybir.AxisListType.X)
            v.tensor_tensor(sm[:, 3:4], sm[:, 0:1], sm[:, 1:2], ALU.add).then_inc(pre_d, 1)
            dve.wait_ge(pre_d, 4)
            v.tensor_tensor(sm[:, 4:5], sm[:, 3:4], sm[:, 2:3], ALU.subtract).then_inc(pre_d, 1)
            dve.wait_ge(pre_p, 3)
            v.tensor_scalar(tmp[:, 1, :], tmp[:, 0, :], sm[:, 5:6], None, ALU.mult).then_inc(pre_d, 1)
            dve.wait_ge(pre_t, 2)
            v.tensor_scalar(ahat, ps[:, 0, 0:P], sm[:, 5:6], None, ALU.mult).then_inc(pre_d, 1)

            def low(o, full, high, scale):
                return v.scalar_tensor_tensor(out=o, in0=full, scalar=scale, in1=high, op0=ALU.mult, op1=ALU.subtract)

            dve.wait_ge(pre_a, 1)
            low(adjh[:, 1, :], adj_t, adjh[:, 0, :], WS)
            pick = cst[:, P:P + 8]
            v.tensor_copy(tmp[:, 0, :], ps[:, 1, 0:P]).then_inc(pre_d, 1)
            dve.wait_ge(ld_misc, 144)
            v.tensor_scalar(tmp[:, 1, :], bgr[:, 0, :], WS, None, ALU.mult).then_inc(pre_d, 1)
            v.tensor_scalar(tmp[:, 2, :], bgr[:, 1, :], WS, None, ALU.mult).then_inc(pre_d, 1)
            v.tensor_tensor(gbias[:], bi[:, 0, :], bi[:, 1, :], ALU.add)
            at, done = 10, 10
            for src, dst, ph, pl, rep in ((tmp[:, 0, :], bias1_x, 0, 1, CB), (tmp[:, 1, :], bias1_w, 2, 3, 1),
                                          (tmp[:, 2, :], bias2_x, 4, 5, CB)):
                dve.wait_ge(pre_d, done)
                v.tensor_copy(tmph[:, 0, :], src).then_inc(pre_d, 1)
                dve.wait_ge(pre_d, done + 1)
                v.tensor_tensor(tmph[:, 1, :], src, tmph[:, 0, :], ALU.subtract).then_inc(pre_d, 1)
                v.tensor_scalar(tmp[:, 3, :], tmph[:, 0, :], pick[:, ph:ph + 1], None, ALU.mult).then_inc(pre_d, 1)
                dve.wait_ge(pre_d, done + 3)
                for b in range(rep):
                    o = dst[:, b, :] if rep > 1 else dst[:]
                    last = v.scalar_tensor_tensor(out=o, in0=tmph[:, 1, :], scalar=pick[:, pl:pl + 1],
                                                  in1=tmp[:, 3, :], op0=ALU.mult, op1=ALU.add)
                last.then_inc(pre_d, 1)
                done += 4
            dve.wait_ge(pre_p, 3)
            v.tensor_scalar(bias2_w[:], zero, pick[:, 6:7], WS, ALU.add, ALU.mult)
            dve.wait_ge(pre_a, 2)
            low(wgh[:, :, 1, :], wg, wgh[:, :, 0, :], WS)

            def turn_a(n):
                for i in range(UNROLL):
                    dve.wait_ge(w_hi, n * UNROLL + (i + 1))
                    dve.wait_ge(z_cp, n * UNROLL + (i + 1))
                    s = bass.ds(n * (UNROLL * WSL) + i * WSL, WSL)
                    low(W[:, :, 1, s], wst[:, :, s], W[:, :, 0, s], WS).then_inc(w_lo, 1)
                    for h in range(HALVES):
                        last = v.bn_stats(stats1[:, h, bass.ds(n * UNROLL + i, 1), :].rearrange("p a s -> p (a s)"),
                                          z[:, h, bass.ds(n * (UNROLL * CH) + i * CH, CH)])
                    last.then_inc(z_st, 1)

            with dve.Fori(0, CHUNKS // UNROLL) as n:
                turn_a(n)

            def batchnorm(stats_done, stats, mv, bn, vec, d, p):
                b, gamma, beta = vec
                dve.wait_ge(stats_done, CHUNKS)
                for h, st in enumerate(stats):
                    last = v.bn_aggr(mv[:, h, :], st)
                last.then_inc(d, 1)
                dve.wait_ge(d, 1)
                v.tensor_scalar(bn[:, 0, :], mv[:, :, 1], EPS, None, ALU.add).then_inc(d, 1)
                v.tensor_tensor(bn[:, 3, :], mv[:, :, 0], b, ALU.add).then_inc(d, 1)
                dve.wait_ge(p, 1)
                v.tensor_tensor(bn[:, 2, :], bn[:, 1, :], gamma, ALU.mult).then_inc(d, 1)
                dve.wait_ge(d, 4)
                v.tensor_tensor(bn[:, 0, :], b, bn[:, 3, :], ALU.subtract).then_inc(d, 1)
                dve.wait_ge(d, 5)
                v.tensor_tensor(bn[:, 1, :], bn[:, 0, :], bn[:, 2, :], ALU.mult).then_inc(d, 1)
                dve.wait_ge(d, 6)
                v.tensor_tensor(bn[:, 3, :], bn[:, 1, :], beta, ALU.add).then_inc(d, 1)

            dve.wait_ge(ld_misc, 144)
            batchnorm(z_st, [stats1[:, h, :, :].rearrange("p k s -> p (k s)") for h in range(HALVES)], mv1, bn1,
                      (v1[:, 0, :], v1[:, 1, :], v1[:, 2, :]), bn1_d, bn1_p)

            with dve.Fori(0, CHUNKS // UNROLL) as n:
                for i in range(UNROLL):
                    dve.wait_ge(o_mm, n * UNROLL + (i + 1))
                    v.tensor_scalar(z[:, 0, bass.ds(n * (UNROLL * CH) + i * CH, CH)], ps[:, i, :], 1.0, None, ALU.mult)
                    v.bn_stats(stats2[:, bass.ds(n * UNROLL + i, 1), :].rearrange("p a s -> p (a s)"),
                               ps[:, i, :]).then_inc(o_cp, 1)

            batchnorm(o_cp, [stats2[:, :, :].rearrange("p k s -> p (k s)")], mv2, bn2,
                      (v2[:, 0:1], v2[:, 1:2], v2[:, 2:3]), bn2_d, bn2_p)
            v.memset(mark[:, GCH:GCH + 1], 0.0).then_inc(y2_d, GCH)

            def norm_stats(t, g, y, j, y_s, y_done, st_s, mv_s):
                dve.wait_ge(y_s, y_done)
                for b in range(CB):
                    last = v.bn_stats(lst[t][:, j, b, :], y[:, b * P:(b + 1) * P])
                last.then_inc(st_s, 1)
                mean_e, m2_e, mean_o, m2_o = (lst[t][:, j, :, k] for k in (1, 2, 4, 5))
                mean, diff, m2, sq, ve = (lmv[t][:, j, k, :] for k in range(5))
                dve.wait_ge(st_s, chunk_no(g, j))
                v.tensor_tensor(diff, mean_e, mean_o, ALU.subtract)
                v.scalar_tensor_tensor(out=m2, in0=m2_e, scalar=P * EPS, in1=m2_o, op0=ALU.add,
                                       op1=ALU.add).then_inc(mv_s, 1)
                dve.wait_ge(mv_s, g * (3 * GCH) + (3 * j + 1))
                v.scalar_tensor_tensor(out=mean, in0=diff, scalar=-0.5 if t == "y" else 0.5, in1=mean_e, op0=ALU.mult,
                                       op1=ALU.add if t == "y" else ALU.subtract)
                v.scalar_tensor_tensor(out=sq, in0=diff, scalar=0.25, in1=diff, op0=ALU.mult,
                                       op1=ALU.mult).then_inc(mv_s, 1)
                dve.wait_ge(mv_s, g * (3 * GCH) + (3 * j + 2))
                v.scalar_tensor_tensor(out=ve, in0=m2, scalar=1.0 / P, in1=sq, op0=ALU.mult,
                                       op1=ALU.add).then_inc(mv_s, 1)

            def norm_apply(t, g, y, o, j, rs_s, o_s):
                dve.wait_ge(rs_s, chunk_no(g, j))
                for b in range(CB):
                    at = slice(b * P, (b + 1) * P)
                    last = v.tensor_scalar(o[:, at], y[:, at], lmv[t][:, j, 0, b:b + 1], lrs[t][:, j, b:b + 1],
                                           ALU.subtract, ALU.mult)
                last.then_inc(o_s, 1)

            def conv_low(g, j, high_s, o_s, o, scalar, op):
                dve.wait_ge(high_s, chunk_no(g, j))
                v.scalar_tensor_tensor(out=o[:, 1, cols(j)], in0=ps[:, j, :], scalar=scalar, in1=o[:, 0, cols(j)],
                                       op0=op, op1=ALU.subtract).then_inc(o_s, 1)

            def turn_c(gw, gx, gy):
                for kind, j, _, g in steps(DVE_ORDER, {"w": gw, "x": gx, "y": gy}):
                    if kind == "ig":
                        u, t = j, j.thread
                        dve.wait_ge(g_a[t], gate_count(g, u, "g"))
                        v.tensor_tensor(gate_buf(u, "g"), gate_buf(u, "i"), gate_buf(u, "g"),
                                        ALU.mult).then_inc(ig_d[t], 1)
                    elif kind == "cell":
                        u, t = j, j.thread
                        dve.wait_ge(ig_d[t], f_no(g, u))
                        dve.wait_ge(fc_p[t], f_no(g, u))
                        v.tensor_tensor(cell[t][:, u.c % 2, 0:u.n], gate_buf(u, "g"), gate_buf(u, "f"),
                                        ALU.add).then_inc(c_d[t], 1)
                    elif kind == "h":
                        u, t = j, j.thread
                        dve.wait_ge(tc_a[t], unit_no(g, u))
                        v.scalar_tensor_tensor(out=gate_buf(u, "g"), in0=gate_buf(u, "o"), scalar=HS,
                                               in1=gate_buf(u, "i"), op0=ALU.mult, op1=ALU.mult).then_inc(h_d[t], 1)
                        dve.wait_ge(h_d[t], unit_no(g, u))
                        v.tensor_copy(h_out(g, u, 0), folded(gate_buf(u, "g"), u)).then_inc(hi_d[t], 1)
                    elif kind == "sum1":
                        dve.wait_ge(tr_t, chunk_no(g, j))
                        dve.wait_ge(ld_xin[j], g * 16 + 16)
                        v.tensor_tensor(xin[:, j, :], ps[:, j, :], xin[:, j, :], ALU.add).then_inc(y_d, 1)
                    elif kind == "stats1":
                        norm_stats("x", g, xin[:, j, :], j, y_d, chunk_no(g, j), st_d, mv_d)
                    elif kind == "agg1":
                        conv_low(g, j, vh_a, vl_d, opB, 1.0 / WS, ALU.mult)
                    elif kind == "lin1":
                        conv_low(g, j, rh_a, rl_d, opA, 0.0, ALU.max)
                    elif kind == "lin2":
                        conv_low(g, j, sh_a, sl_d, opB, 1.0 / (WS * WS), ALU.mult)
                    elif kind == "agg2":
                        conv_low(g, j, h0h_a, h0l_d, opA, 0.0, ALU.max)
                    elif kind == "sum2":
                        dve.wait_ge(fin_t, chunk_no(g, j))
                        if j >= 2:
                            dve.wait_ge(o_d, chunk_no(g, j - 2))
                        v.tensor_tensor(y2[:, j % 2, :], ps[:, bank0["y"] + j, :], x1[:, g % 3, cols(j)],
                                        ALU.add).then_inc(y2_d, 1)
                    elif kind == "stats2":
                        norm_stats("y", g, y2[:, j % 2, :], j, y2_d, g * GCH + (GCH + j + 1), st2_d, mv2_d)
                    elif kind == "store":
                        norm_apply("y", g, y2[:, j % 2, :], x1[:, g % 3, cols(j)], j, rs2_p, o_d)

            turns(dve, turn_c)

        @block.gpsimd
        def _(pool):
            gp = nc.gpsimd
            gp.memset(minus_half[:], -0.5).then_inc(pre_p, 1)
            gp.memset(zero, 0.0)
            for j in range(GCH):
                gp.memset(mark[:, j:j + 1], 0.0).then_inc(stored[j], 16)
            gp.memset(ones, 1.0).then_inc(pre_p, 1)
            pool.wait_ge(pre_p, 2)
            pool.wait_ge(pre_d, 5)
            gp.tensor_tensor(sm[:, 5:6], sm[:, 4:5], minus_half[:, 0:1], ALU.pow).then_inc(pre_p, 1)
            for bn, h, d, p in ((bn1, HALVES, bn1_d, bn1_p), (bn2, 1, bn2_d, bn2_p)):
                pool.wait_ge(d, 2)
                gp.tensor_tensor(bn[:, 1, :], bn[:, 0, :], minus_half[:, 0:h], ALU.pow).then_inc(p, 1)

            def rstd(t, g, j, mv_s, rs_s):
                pool.wait_ge(mv_s, g * (3 * GCH) + 3 * (j + 1))
                gp.tensor_tensor(lrs[t][:, j, :], lmv[t][:, j, 4, :], minus_half[:], ALU.pow).then_inc(rs_s, 1)
                if t == "x":
                    pool.wait_ge(rs_s, g * (2 * GCH) + (2 * j + 1))
                    gp.tensor_tensor(nmr[:, j, :], lmv[t][:, j, 0, :], lrs[t][:, j, :], ALU.mult).then_inc(rs_s, 1)

            def turn_c(gw, gx, gy):
                for kind, j, _, g in steps(POOL_ORDER, {"w": gw, "x": gx, "y": gy}):
                    if kind == "c1":
                        u, t = j, j.thread
                        pool.wait_ge(g_a[t], gate_count(g, u, "g"))
                        gp.tensor_tensor(cell[t][:, u.c % 2, 0:u.n], gate_buf(u, "i"), gate_buf(u, "g"),
                                         ALU.mult).then_inc(c1_p[t], 1)
                    elif kind == "fc":
                        u, t = j, j.thread
                        pool.wait_ge(g_a[t], gate_count(g, u, "f"))
                        gp.tensor_tensor(gate_buf(u, "f"), gate_buf(u, "f"), cell[t][:, u.c % 2, 0:u.n],
                                         ALU.mult).then_inc(fc_p[t], 1)
                    elif kind == "h":
                        u, t = j, j.thread
                        pool.wait_ge(hi_d[t], unit_no(g, u))
                        gp.tensor_tensor(h_out(g, u, 1), folded(gate_buf(u, "g"), u), h_out(g, u, 0),
                                         ALU.subtract).then_inc(lo_p[t], 1)
                    elif kind == "rstd1":
                        rstd("x", g, j, mv_d, rs_p)
                    elif kind == "x1":
                        pool.wait_ge(x1h_a, chunk_no(g, j))
                        gp.tensor_tensor(opA[:, 1, cols(j)], x1[:, g % 3, cols(j)], opA[:, 0, cols(j)],
                                         ALU.subtract).then_inc(x1l_p, 1)
                    elif kind == "rstd2":
                        rstd("y", g, j, mv2_d, rs2_p)

            turns(pool, turn_c)


def kernel(**inputs):
    import numpy as _np
    import concourse.bacc as _bacc
    from concourse import mybir as _mybir
    from concourse.bass_utils import run_bass_kernel_spmd as _run

    a = {k: _np.asarray(v) for k, v in inputs.items()}

    def column(v, n):
        return v.reshape(n, P).T

    consts = _np.zeros((P, P + 8), _np.float32)
    consts[:, :P] = _np.eye(P)
    for c, rows in enumerate(((0, 2), (1, 3), (0, 1), (2, 3), (0,), (1,), (0, 1))):
        consts[list(rows), P + c] = 1.0

    host = {
        "xn": a["x"].transpose(1, 0, 2).reshape(P, COLS),
        "adj": a["adj"],
        "adjT": a["adj"].T,
        "W1T": a["L0_gnn_W1"].T,
        "W2T": a["L0_gnn_W2"].T.reshape(HALVES, P, P).transpose(1, 0, 2),
        "vec1": _np.stack([column(a[f"L0_gnn_{n}"], HALVES) for n in ("b1", "g1", "be1")], 1),
        "vec2": _np.stack([a[f"L0_gnn_{n}"] for n in ("b2", "g2", "be2")], 1),
        "Wg0": a["L1_gnn_Wg0"],
        "Wg1": a["L1_gnn_Wg1"],
        "bg0": _np.broadcast_to(a["L1_gnn_bg0"], (P, P)),
        "bg1": _np.broadcast_to(a["L1_gnn_bg1"], (P, P)),
        "WihT": a["L1_gnn_Wih"].transpose(2, 0, 1).reshape(P, -1),
        "WhhT": a["L1_gnn_Whh"].transpose(2, 0, 1).reshape(P, -1),
        "bih": column(a["L1_gnn_bih"].reshape(-1), MAX_SKIP * 4),
        "bhh": column(a["L1_gnn_bhh"].reshape(-1), MAX_SKIP * 4),
        "consts": consts,
    }
    nc = _bacc.Bacc("TRN2", target_bir_lowering=False, num_devices=1)
    arrays, args = {}, []
    for name, v in host.items():
        v = _np.ascontiguousarray(v)
        arrays[f"in_{name}_dram"] = v
        args.append(nc.dram_tensor(f"in_{name}_dram", v.shape, _mybir.dt.from_np(v.dtype), kind="ExternalInput").ap())
    args.append(nc.dram_tensor("out_dram", (P, COLS), F32, kind="ExternalOutput").ap())
    gnn_kernel(nc, *args)
    r = _run(nc, [arrays], core_ids=[0])
    got = r.results[0]["out_dram"]
    return _np.ascontiguousarray(got.reshape(P, B, P).transpose(1, 0, 2))
```

```python
from collections import namedtuple
from contextlib import ExitStack

import concourse.bass as bass
from concourse import mybir

F32 = mybir.dt.float32
F16 = mybir.dt.float16
ALU = mybir.AluOpType
ACT = mybir.ActivationFunctionType

P = 128
B = 128
HID = 256
HALVES = HID // P
COLS = B * P
CB = 4
CH = CB * P
CHUNKS = B // CB
UNROLL = 4
GB = 16
GC = GB * P
GCH = GB // CB
GROUPS = B // GB
EPS = 1e-5

WS = 64.0
HS = 256.0
MAX_SKIP = 4
WSL = MAX_SKIP * 4 * P // CHUNKS
GATE = {"i": 0, "f": 1, "g": 2, "o": 3}
BANK = {"i": 0, "g": 1, "f": 2, "o": 3}

WARM_LOAD, WARM_DEGREES, WARM_AHAT, WARM_NORM1, WARM_NORM2 = 12,9,6,27,17
BANK_GATE = "igfo"

Unit = namedtuple("Unit", "thread p s c b0 nb nw n k gate0")


def lstm_units(thread, plan):
    units, gate0 = [], 0
    for k, (p, s, c, b0, nb) in enumerate(plan):
        nw = P // p
        units.append(Unit(thread, p, s, c, b0, nb, nw, nb * nw, k, gate0))
        gate0 += 3 if s == 1 else 4
    return units, gate0


HALF = GB // 2
X_PLAN = ([(1, 1, j, CB * j, CB) for j in range(GCH)]
          + [(2, s, c, HALF * c, HALF) for s in (1, 2) for c in range(2)])
Y_PLAN = [(p, s, c, HALF * c, HALF) for p in (3, 4) for s in range(1, p + 1) for c in range(2)]
X_UNITS, X_GATES = lstm_units("x", X_PLAN)
Y_UNITS, Y_GATES = lstm_units("y", Y_PLAN)
X_LAST = lstm_units("x", X_PLAN + Y_PLAN)[0]
NX, NY = len(X_UNITS), len(Y_UNITS)


def unit(p, s, c, thread=None):
    units = X_LAST if thread == "x" else Y_UNITS if thread == "y" else X_UNITS + Y_UNITS
    return next(u for u in units if (u.p, u.s, u.c) == (p, s, c))


def gates(u):
    return "igo" if u.s == 1 else "figo"


def gate_no(u, q):
    return u.gate0 + gates(u).index(q) + 1


PE_FIRST = """
    norm1.0- norm1.1- norm1.2- norm1.3- warm.9 warm.9 agg1.0 lin1.0 agg1.1 norm1.0 agg1.2 lin1.1 lin2.0 lin1.2 norm1.1 agg1.3
    agg2.0 norm1.2 lin2.1 lin1.3 lin2.2 agg2.1 input.110 norm1.3 agg2.2 input.111 lin2.3 input.112 agg2.3
    input.113 input.210 input.211 input.220 hidden.220 input.221 hidden.221"""
PE_LOOP = """
    agg1.0 agg1.1 agg1.2 agg1.3 input.310 input.311 input.320 lin1.0 lin1.1 lin1.2 norm1.0 hidden.320 lin2.0
    norm1.1 input.321 hidden.321 lin1.3 norm1.2 input.330 hidden.330 norm1.3 input.331 hidden.331 lin2.1 lin2.2
    input.410 agg2.0 lin2.3 input.411 agg2.1 input.420 agg2.2 hidden.420 agg2.3 input.421 hidden.421 input.430
    input.110 hidden.430 input.111 input.431 hidden.431 input.112 input.113 input.440 hidden.440 input.210
    input.441 hidden.441 input.211 norm2.0 norm2.1 input.220 hidden.220 norm2.2 input.221 hidden.221 norm2.3"""
PE_LAST = """
    agg1.0 agg1.1 agg1.2 agg1.3 input.310 input.311 input.320 lin1.0 lin1.1 lin1.2 lin2.0 hidden.320 lin2.1
    lin1.3 input.321 hidden.321 lin2.2 agg2.0 lin2.3 agg2.1 agg2.2 input.330 agg2.3 hidden.330 input.110
    input.111 input.112 input.113 input.331 hidden.331 input.210 input.211 input.410 input.220 input.411
    hidden.220 input.420 input.221 hidden.420 hidden.221 input.421 hidden.421 input.310+ input.430 hidden.430
    input.311+ input.320+ hidden.320+ input.321+ hidden.321+ input.431 hidden.431 input.330+ hidden.330+
    input.331+ hidden.331+ input.440 hidden.440 input.410+ input.441 hidden.441 input.411+ norm2.0 norm2.1
    input.420+ hidden.420+ input.421+ hidden.421+ input.430+ hidden.430+ norm2.2 norm2.3 input.431+ hidden.431+
    input.440+ hidden.440+ input.441+ hidden.441+ norm2.0+ norm2.1+ norm2.2+ norm2.3+"""
ACT_FIRST = """
    yT.0- yT.1- yT.2- yT.3- yT.0 yT.1 apply1.0- applied.0- x1.0- apply1.1- applied.1- x1.1- agg1.0 apply1.2-
    applied.2- x1.2- lin1.0 agg1.1 apply1.3- agg1.2 applied.3- x1.3- lin1.1 lin2.0 lin1.2 yT.2 agg1.3 agg2.0
    lin2.1 yT.3 lin1.3 lin2.2 agg2.1 gates.110.igo agg2.2 tanh.110 gates.111.igo lin2.3 apply1.0 applied.0
    gates.112.i agg2.3 gates.112.go tanh.111 gates.113.ig tanh.112 gates.113.o x1.0 tanh.113 apply1.1 applied.1
    gates.210.igo x1.1 tanh.210 gates.211.igo apply1.2 applied.2 x1.2 gates.220.f tanh.211 gates.220.igo
    apply1.3 tanh.220 applied.3 gates.221.figo x1.3 tanh.221"""
ACT_LOOP = """
    agg1.0 agg1.1 yT.0 gates.310.igo gates.311.igo agg1.2 tanh.310 tanh.311 lin1.0 yT.1 lin1.1 gates.320.f
    lin1.2 agg1.3 gates.320.igo lin2.0 yT.2 tanh.320 apply1.0 applied.0 gates.321.figo lin1.3 tanh.321 yT.3
    gates.330.figo apply1.1 tanh.330 applied.1 gates.331.figo lin2.1 tanh.331 gates.410.ig lin2.2 agg2.0
    gates.410.o lin2.3 tanh.410 gates.411.igo agg2.1 apply1.2 applied.2 gates.420.f tanh.411 gates.420.igo
    agg2.2 agg2.3 tanh.420 gates.421.figo apply1.3 applied.3 gates.110.ig tanh.421 gates.110.o gates.430.figo
    gates.111.ig tanh.110 tanh.430 gates.111.o gates.431.fig tanh.111 gates.112.ig gates.431.o gates.112.o
    gates.113.ig tanh.431 gates.113.o tanh.112 gates.440.f tanh.113 gates.440.ig gates.210.ig gates.440.o
    gates.210.o tanh.440 gates.441.fig tanh.210 x1.0 gates.441.o tanh.441 gates.211.igo x1.1 tanh.211
    gates.220.fi x1.2 x1.3 gates.220.go gates.221.fig tanh.220 gates.221.o tanh.221"""
ACT_LAST = """
    agg1.0 gates.310.igo gates.311.igo agg1.1 agg1.2 agg1.3 tanh.310 lin1.0 lin1.1 lin1.2 tanh.311 gates.320.f
    lin2.0 gates.320.igo lin2.1 lin1.3 gates.321.fig tanh.320 lin2.2 agg2.0 lin2.3 agg2.1 gates.321.o agg2.2
    agg2.3 gates.330.fig tanh.321 gates.330.o gates.110.igo gates.111.ig tanh.110 gates.111.o gates.112.ig
    tanh.111 gates.112.o gates.113.ig tanh.112 gates.113.o tanh.113 gates.331.fig gates.210.i tanh.330
    gates.210.go gates.331.o gates.211.ig tanh.331 gates.410.i tanh.210 gates.211.o gates.410.go tanh.410
    gates.411.i gates.220.f gates.411.go gates.220.i tanh.211 gates.220.g tanh.411 gates.220.o gates.420.fig
    tanh.220 gates.221.fig gates.420.o gates.221.o tanh.420 tanh.221 gates.421.fig gates.310+.i gates.421.o
    gates.310+.g tanh.310+ gates.310+.o gates.430.f gates.311+.igo tanh.421 tanh.311+ gates.320+.f gates.430.i
    gates.320+.igo gates.430.go gates.321+.f tanh.430 tanh.320+ gates.321+.igo gates.431.fi tanh.321+
    gates.431.g gates.330+.fig tanh.431 gates.330+.o gates.431.o tanh.330+ gates.331+.figo tanh.331+
    gates.440.fig gates.410+.ig gates.440.o tanh.440 tanh.410+ gates.410+.o gates.441.fig gates.411+.igo
    gates.441.o tanh.411+ tanh.441 gates.420+.figo gates.421+.f tanh.420+ gates.421+.igo tanh.421+
    gates.430+.figo tanh.430+ gates.431+.figo gates.440+.figo tanh.431+ tanh.440+ gates.441+.figo tanh.441+"""
DVE_FIRST = """
    sum1.0- stats1.0- sum1.1- stats1.1- sum1.2- sum1.3- stats1.2- stats1.3- agg1.0 lin1.0 agg1.1 sum1.0 agg1.2
    lin1.1 lin2.0 lin1.2 sum1.1 agg1.3 sum1.2 agg2.0 lin2.1 stats1.0 lin1.3 lin2.2 agg2.1 sum1.3 stats1.1 agg2.2
    stats1.2 lin2.3 h.110 agg2.3 h.111 h.112 h.113 stats1.3 h.210 h.211 ig.220 cell.220 h.220 ig.221 cell.221
    h.221"""
DVE_LOOP = """
    agg1.0 agg1.1 agg1.2 h.310 lin1.0 h.311 lin1.1 sum1.0 stats1.0 ig.320 cell.320 agg1.3 sum1.1 lin1.2 h.320
    stats1.1 ig.321 cell.321 lin1.3 h.321 sum1.2 lin2.0 ig.330 cell.330 stats1.2 h.330 ig.331 cell.331 sum1.3
    h.331 lin2.1 agg2.0 lin2.2 h.410 stats1.3 agg2.1 lin2.3 h.411 ig.420 cell.420 agg2.2 agg2.3 ig.421 cell.421
    h.420 h.421 ig.430 cell.430 h.110 h.430 ig.431 h.111 cell.431 h.431 h.112 h.113 ig.440 cell.440 h.440 ig.441
    cell.441 h.210 h.441 sum2.0 sum2.1 stats2.0 stats2.1 h.211 store.0 store.1 ig.220 sum2.2 cell.220 stats2.2
    ig.221 sum2.3 cell.221 h.220 h.221 stats2.3 store.2 store.3"""
DVE_LAST = """
    agg1.0 agg1.1 agg1.2 h.310 lin1.0 lin1.1 lin1.2 agg1.3 h.311 lin1.3 ig.320 cell.320 lin2.0 lin2.1 h.320
    lin2.2 ig.321 agg2.0 lin2.3 agg2.1 agg2.2 agg2.3 cell.321 ig.330 cell.330 h.321 h.110 h.111 h.112 h.113
    h.330 ig.331 cell.331 h.331 h.210 h.410 ig.220 h.211 cell.220 h.411 ig.420 h.220 cell.420 ig.221 cell.221
    h.420 h.221 ig.421 cell.421 h.310+ h.421 h.311+ ig.430 cell.430 ig.320+ cell.320+ ig.321+ cell.321+ h.320+
    h.430 ig.431 cell.431 h.321+ ig.330+ cell.330+ h.330+ h.431 ig.331+ cell.331+ h.331+ ig.440 cell.440 h.440
    h.410+ ig.441 cell.441 sum2.0 sum2.1 h.411+ stats2.0 ig.420+ h.441 cell.420+ stats2.1 ig.421+ h.420+
    cell.421+ store.0 store.1 h.421+ ig.430+ sum2.2 cell.430+ sum2.3 h.430+ stats2.2 ig.431+ stats2.3 cell.431+
    ig.440+ cell.440+ h.431+ h.440+ store.2 store.3 ig.441+ sum2.0+ sum2.1+ cell.441+ stats2.0+ h.441+ stats2.1+
    store.0+ store.1+ sum2.2+ sum2.3+ stats2.2+ stats2.3+ store.2+ store.3+"""
POOL_FIRST = """
    rstd1.0- rstd1.1- x1.0- rstd1.2- x1.1- rstd1.3- x1.2- x1.3- rstd1.0 c1.110 c1.111 rstd1.1 rstd1.2 h.110
    c1.112 c1.113 h.111 h.112 h.113 c1.210 x1.0 h.210 c1.211 rstd1.3 fc.220 h.211 x1.1 x1.2 fc.221 h.220 x1.3
    h.221"""
POOL_LOOP = """
    c1.310 c1.311 h.310 fc.320 h.311 rstd1.0 h.320 fc.321 rstd1.1 fc.330 h.321 fc.331 h.330 rstd1.2 h.331 c1.410
    c1.411 h.410 rstd1.3 fc.420 h.411 fc.421 h.420 fc.430 c1.110 h.421 c1.111 h.110 h.430 fc.431 h.111 c1.112
    c1.113 h.431 fc.440 h.112 h.113 c1.210 fc.441 h.440 x1.0 h.210 h.441 c1.211 x1.1 rstd2.0 rstd2.1 h.211
    fc.220 x1.2 fc.221 rstd2.2 x1.3 h.220 h.221 rstd2.3"""
POOL_LAST = """
    c1.310 h.310 c1.311 h.311 fc.320 fc.321 h.320 fc.330 c1.110 h.321 c1.111 h.110 c1.112 c1.113 h.111 h.112
    h.113 fc.331 h.330 c1.210 h.331 h.210 c1.410 c1.211 c1.411 h.410 fc.220 h.211 fc.420 h.411 fc.221 h.220
    h.420 fc.421 h.221 c1.310+ h.310+ c1.311+ fc.430 h.311+ h.421 fc.320+ fc.321+ fc.431 h.320+ fc.330+ h.321+
    h.430 fc.331+ h.330+ h.431 fc.440 c1.410+ h.331+ h.440 fc.441 c1.411+ h.410+ fc.420+ h.411+ rstd2.0 fc.421+
    rstd2.1 h.420+ h.441 fc.430+ h.421+ h.430+ fc.431+ fc.440+ rstd2.2 rstd2.3 h.431+ h.440+ fc.441+ rstd2.0+
    h.441+ rstd2.1+ rstd2.2+ rstd2.3+"""
PE_ORDERS = PE_FIRST, PE_LOOP, PE_LAST
ACT_ORDERS = ACT_FIRST, ACT_LOOP, ACT_LAST
DVE_ORDERS = DVE_FIRST, DVE_LOOP, DVE_LAST
POOL_ORDERS = POOL_FIRST, POOL_LOOP, POOL_LAST
THREAD = {"yT": "w", "norm1": "w", "sum1": "w", "stats1": "w", "rstd1": "w", "apply1": "w", "applied": "w", "x1": "w",
          "norm2": "y", "sum2": "y", "stats2": "y", "rstd2": "y", "store": "y"}


def steps(order, groups):
    for step in order.split():
        kind, where, *some = step.split(".")
        shift = {"-": -1, "+": 1}.get(where[-1], 0)
        where = where.rstrip("+-")
        if len(where) == 1:
            item, g = int(where), groups[THREAD.get(kind, "x")]
        elif shift:
            item, g = unit(*(int(c) for c in where), "x"), groups["y"]
        else:
            item = unit(*(int(c) for c in where))
            g = groups[item.thread]
        yield kind, item, some[0] if some else "", g + shift


def gnn_kernel(nc, xn, adj, adjT, W1T, W2T, vec1, vec2, Wg0, Wg1, bg0, bg1, WihT, WhhT, bih, bhh,
               consts, out):
    ctx = ExitStack()
    with ctx:
        def sb(name, shape, dt=F32):
            return ctx.enter_context(nc.sbuf_tensor(name, shape, dt))

        def sem(name):
            return ctx.enter_context(nc.semaphore(name))

        z = sb("z", [P, HALVES, COLS])
        late = z[:, 1, :]

        def carve(at, n, dt=F32):
            return late[:, at:at + n] if dt is F32 else late[:, at:at + n].bitcast(dt)

        x1 = carve(0, 3 * GC).rearrange("p (t c) -> p t c", t=3)
        opA = carve(6144, GC, F16).rearrange("p (l c) -> p l c", l=2)
        opB = carve(8192, GC, F16).rearrange("p (l c) -> p l c", l=2)
        H = carve(10240, 2 * GC, F16).rearrange("p (t l c) -> p t l c", t=2, l=2)
        xin = carve(14336, GCH * CH).rearrange("p (j c) -> p j c", j=GCH)

        gbuf = {t: sb(f"gbuf_{t}", [P, 2, 4, CH]) for t in "xy"}
        gbuf3 = {t: z[:, 0, i * GC:(i + 1) * GC].rearrange("p (q c) -> p q c", q=4) for i, t in enumerate("xy")}
        cell = {t: sb(f"cell_{t}", [P, 2, CH]) for t in "xy"}
        hst = {t: sb(f"hst_{t}", [P, 2, 2, CH], F16) for t in "xy"}
        wst = gbuf["x"][:, :, :, :].rearrange("p a q c -> p (a q c)").rearrange("p (m c) -> p m c", m=2)
        W = sb("W", [P, 2, 2, MAX_SKIP * 4 * P], F16)
        xa = gbuf["y"][:, :, :, :].rearrange("p a q c -> p (a q) c")
        x_ring = xa[:, 0:4, :]
        agg = xa[:, 4:6, :].rearrange("p a c -> p (a c)").bitcast(F16).rearrange("p (a l c) -> p a l c", a=2, l=2)
        early = cell["x"][:, :, :].rearrange("p a (q c) -> p (a q) c", c=P)
        tmp, ones, zero = early[:, 0:4, :], early[:, 4, :], early[:, 5, :]
        early = cell["y"][:, :, :].rearrange("p a (q c) -> p (a q) c", c=P)
        adj_n, adj_t, wg, bgr = early[:, 0, :], early[:, 1, :], early[:, 2:4, :], early[:, 4:6, :]
        ahat = early[:, 6, :]
        early = hst["x"][:, :, :, :].rearrange("p a l c -> p (a l c)").bitcast(F32)
        w1, w2 = early[:, 0:HID], early[:, HID:2 * HID].rearrange("p (h c) -> p h c", h=HALVES)
        w1h = early[:, 2 * HID:3 * HID].bitcast(F16).rearrange("p (l r) -> p l r", l=2)
        v1 = sb("v1", [P, 3, HALVES])
        v2 = sb("v2", [P, 3])
        cst = sb("cst", [P, P + 8])
        ident = cst[:, 0:P]
        bi = sb("bi", [P, 2, MAX_SKIP * 4])
        gbias = sb("gbias", [P, MAX_SKIP * 4])
        adjh = sb("adjh", [P, 2, P], F16)
        wgh = sb("wgh", [P, 2, 2, P], F16)
        idh = sb("idh", [P, P], F16)
        bias1_w = sb("bias1_w", [P, P], F16)
        bias1_x = sb("bias1_x", [P, CB, P], F16)
        bias2_w = sb("bias2_w", [P, P], F16)
        bias2_x = sb("bias2_x", [P, CB, P], F16)
        tmph = sb("tmph", [P, 2, P], F16)
        minus_half = sb("minus_half", [P, CB])
        sm = sb("sm", [P, 6])
        warm = sb("warm", [P, 1])
        mark = sb("mark", [P, GCH + 1])
        early = hst["y"][:, :, :, :].rearrange("p a l c -> p (a l c)").bitcast(F32)
        stats1 = early[:, 0:HALVES * CHUNKS * 6].rearrange("p (h k s) -> p h k s", h=HALVES, k=CHUNKS)
        stats2 = stats1[:, 0, :, :]
        mv1 = sb("mv1", [P, HALVES, 2])
        mv2 = sb("mv2", [P, 1, 2])
        bn1 = sb("bn1", [P, 4, HALVES])
        bn2 = sb("bn2", [P, 4, 1])
        lst = {t: sb(f"lst_{t}", [P, GCH, CB, 6]) for t in "xy"}
        lmv = {t: sb(f"lmv_{t}", [P, GCH, 5, CB]) for t in "xy"}
        lrs = {t: sb(f"lrs_{t}", [P, GCH, CB]) for t in "xy"}
        nmr = sb("nmr", [P, GCH, CB])
        yT = sb("yT", [P, 2, CH])
        y2 = sb("y2", [P, 2, CH])

        ps = ctx.enter_context(nc.psum_tensor("ps", [P, 8, CH], F32))
        bank0 = {"x": 0, "y": 4}

        ld_adj, ld_w1, ld_misc, ld_lstm = sem("ld_adj"), sem("ld_w1"), sem("ld_misc"), sem("ld_lstm")
        ld_x = [sem(f"ld_x{i}") for i in range(UNROLL)]
        ld_xin = [sem(f"ld_xin{i}") for i in range(GCH)]
        pre_d, pre_a, pre_p, pre_t = sem("pre_d"), sem("pre_a"), sem("pre_p"), sem("pre_t")
        w_hi, w_lo = sem("w_hi"), sem("w_lo")
        w1_lo = sem("w1_lo")
        agg_mm, agg_hi, agg_lo = sem("agg_mm"), sem("agg_hi"), sem("agg_lo")
        z_mm, z_cp, z_st = sem("z_mm"), sem("z_cp"), sem("z_st")
        bn1_d, bn1_p = sem("bn1_d"), sem("bn1_p")
        r_act, o_mm, o_cp = sem("r_act"), sem("o_mm"), sem("o_cp")
        bn2_d, bn2_p = sem("bn2_d"), sem("bn2_p")
        yT_a, tr_t, y_d, st_d, mv_d, rs_p, x1_a, x1h_a, x1l_p = (
            sem(n) for n in ("yT_a", "tr_t", "y_d", "st_d", "mv_d", "rs_p", "x1_a", "x1h_a", "x1l_p"))
        agg1_t, lin1_t, lin2_t, agg2_t = (sem(n) for n in ("agg1_t", "lin1_t", "lin2_t", "agg2_t"))
        vh_a, rh_a, sh_a, h0h_a = (sem(n) for n in ("vh_a", "rh_a", "sh_a", "h0h_a"))
        vl_d, rl_d, sl_d, h0l_d = (sem(n) for n in ("vl_d", "rl_d", "sl_d", "h0l_d"))
        fin_t, y2_d, st2_d, mv2_d, rs2_p, o_d = (
            sem(n) for n in ("fin_t", "y2_d", "st2_d", "mv2_d", "rs2_p", "o_d"))
        stored = [sem(f"stored{j}") for j in range(GCH)]
        g_t = {t: sem(f"g_t_{t}") for t in "xy"}
        g_a = {t: sem(f"g_a_{t}") for t in "xy"}
        ig_d = {t: sem(f"ig_d_{t}") for t in "xy"}
        fc_p = {t: sem(f"fc_p_{t}") for t in "xy"}
        c1_p = {t: sem(f"c1_p_{t}") for t in "xy"}
        c_d = {t: sem(f"c_d_{t}") for t in "xy"}
        tc_a = {t: sem(f"tc_a_{t}") for t in "xy"}
        h_d = {t: sem(f"h_d_{t}") for t in "xy"}
        hi_d = {t: sem(f"hi_d_{t}") for t in "xy"}
        lo_p = {t: sem(f"lo_p_{t}") for t in "xy"}

        UNITS = {"x": NX, "y": NY}
        NGATES = {"x": X_GATES, "y": Y_GATES}

        def chunk_no(g, j):
            return g * GCH + (j + 1)

        def unit_no(g, u):
            return g * UNITS[u.thread] + (u.k + 1)

        def gate_count(g, u, q):
            return g * NGATES[u.thread] + gate_no(u, q)

        def step_no(g, u, first):
            units, so_far = (X_UNITS, X_LAST) if u.thread == "x" else (Y_UNITS, Y_UNITS)
            return g * sum((w.s == 1) == first for w in units) + sum((w.s == 1) == first for w in so_far[:u.k + 1])

        def first_no(g, u):
            return step_no(g, u, True)

        def f_no(g, u):
            return step_no(g, u, False)

        def before(u):
            return (X_LAST if u.thread == "x" else Y_UNITS)[u.k - 1]

        def cols(j):
            return slice(j * CH, (j + 1) * CH)

        def windows(hp, u, t):
            v = hp.rearrange("p (b t) -> p b t", t=P)
            return v[:, u.b0:u.b0 + u.nb, t:t + u.p * (u.nw - 1) + 1:u.p]

        def folded(ap, u):
            return ap.rearrange("p (b w) -> p b w", w=u.nw)

        def gate_buf(u, q):
            slot = gbuf3[u.thread] if u.k % 3 == 2 else gbuf[u.thread][:, u.k % 3, :, :]
            return slot[:, BANK[q], 0:u.n]

        def gate_bank(g, u, q):
            return ps[:, (bank0["y"] if isinstance(g, int) and g == 0 else bank0[u.thread]) + BANK[q], 0:u.n]

        def h_out(g, u, part):
            if u.s == u.p:
                return windows(H[:, g % 2, part, :], u, u.p - 1)
            return folded(hst[u.thread][:, u.c, part, 0:u.n], u)

        block = ctx.enter_context(nc.Block())

        def turns(eng, body, orders):
            first, loop, last = orders
            body(first, 1, 0, None)
            with eng.Fori(1, GROUPS - 1) as g:
                body(loop, g + 1, g, g - 1)
            body(last, None, GROUPS - 1, GROUPS - 2)

        def late(g):
            return isinstance(g, int) and g == GROUPS - 1

        @block.sync
        def _(sp):
            for dst, src in ((adj_n, adj), (adj_t, adjT), (cst[:], consts)):
                sp.dma_start(dst, src).then_inc(ld_adj, 16)
            sp.dma_start(w1, W1T).then_inc(ld_w1, 16)
            for i in range(UNROLL):
                sp.dma_start(x_ring[:, i, :], xn[:, cols(i)]).then_inc(ld_x[i], 16)
            for dst, src in ((v1[:], vec1), (v2[:], vec2), (w2, W2T), (wg[:, 0, :], Wg0), (wg[:, 1, :], Wg1),
                             (bgr[:, 0, :], bg0), (bgr[:, 1, :], bg1), (bi[:, 0, :], bih), (bi[:, 1, :], bhh)):
                sp.dma_start(dst, src).then_inc(ld_misc, 16)
            sp.dma_start(wst[:, 0, :], WihT).then_inc(ld_lstm, 16)
            sp.dma_start(wst[:, 1, :], WhhT).then_inc(ld_lstm, 16)
            with sp.Fori(1, CHUNKS // UNROLL) as n:
                for i in range(UNROLL):
                    sp.wait_ge(agg_mm, (n - 1) * UNROLL + (i + 1))
                    sp.dma_start(x_ring[:, i, :], xn[:, bass.ds(n * (UNROLL * CH) + i * CH, CH)]).then_inc(ld_x[i], 16)

            sp.wait_ge(o_mm, CHUNKS)
            for j in range(GCH):
                sp.dma_start(xin[:, j, :], xn[:, cols(j)]).then_inc(ld_xin[j], 16)

            def load(g):
                for j in range(GCH):
                    sp.wait_ge(x1_a, g * GCH - (GCH - 1) + j)
                    sp.dma_start(xin[:, j, :], xn[:, bass.ds(g * GC + j * CH, CH)]).then_inc(ld_xin[j], 16)

            def store(g):
                for j in range(GCH):
                    sp.wait_ge(o_d, chunk_no(g, j))
                    sp.dma_start(out[:, bass.ds(g * GC + j * CH, CH)], x1[:, g % 3, cols(j)]).then_inc(stored[j], 16)

            load(1)
            with sp.Fori(1, GROUPS - 1) as g:
                load(g + 1)
                store(g - 1)
            store(GROUPS - 2)
            store(GROUPS - 1)
            for j in range(GCH):
                sp.wait_ge(stored[j], 16 * (GROUPS + 1))

        @block.tensor
        def _(pe):
            def mm(o, w, m, start, stop):
                return pe.matmul(o, w, m, start=start, stop=stop, skip_group_check=True)

            def keep_warm(stat, mov, times):
                for _ in range(times):
                    mm(ps[:, 7, 0:mov.shape[-1]], stat, mov, True, True)

            pe.wait_ge(pre_p, 2)
            keep_warm(ones, ones, WARM_LOAD)
            pe.wait_ge(ld_adj, 48)
            mm(ps[:, 1, 0:P], ones, adj_t, True, True).then_inc(pre_t, 1)
            keep_warm(ones, ones, WARM_DEGREES)
            pe.wait_ge(pre_d, 6)
            pe.transpose(ps[:, 0, 0:P], tmp[:, 1, :], ident).then_inc(pre_t, 1)
            keep_warm(ones, ones, WARM_AHAT)
            pe.wait_ge(pre_d, 8)

            def aggregate(n, i):
                k = n * UNROLL + i
                pe.wait_ge(ld_x[i], n * 16 + 16)
                if not (isinstance(k, int) and k < 2):
                    pe.wait_ge(agg_lo, k - 1)
                for b in range(CB):
                    last = mm(ps[:, i % 2, b * P:(b + 1) * P], x_ring[:, i, b * P:(b + 1) * P], ahat, True, True)
                last.then_inc(agg_mm, 1)

            def hidden(n, i):
                k = n * UNROLL + i
                if isinstance(k, int) and k == 0:
                    pe.wait_ge(w1_lo, 1)
                pe.wait_ge(agg_lo, k + 1)
                if not (isinstance(k, int) and k < 2):
                    pe.wait_ge(z_cp, k - 1)
                for h in range(HALVES):
                    o = ps[:, 2 + 2 * (i % 2) + h, :]
                    w = [w1h[:, part, h * P:(h + 1) * P] for part in range(2)]
                    mm(o, w[0], agg[:, i % 2, 0, :], True, False)
                    mm(o, w[1], agg[:, i % 2, 0, :], False, False)
                    last = mm(o, w[0], agg[:, i % 2, 1, :], False, True)
                last.then_inc(z_mm, 1)

            def turn_a(n):
                for i in range(UNROLL):
                    aggregate(n, i)
                    if not (isinstance(n, int) and i == 0):
                        hidden(n, i - 1)

            turn_a(0)
            with pe.Fori(1, CHUNKS // UNROLL) as n:
                turn_a(n)
            hidden(CHUNKS // UNROLL, -1)

            def turn_b(n):
                for i in range(UNROLL):
                    k = n * UNROLL + i
                    if not isinstance(n, int):
                        pe.wait_ge(o_cp, k - (UNROLL - 1))
                    for h in range(HALVES):
                        pe.wait_ge(r_act, k * HALVES + (h + 1))
                        last = mm(ps[:, i, :], w2[:, h, :], z[:, h, bass.ds(n * (UNROLL * CH) + i * CH, CH)],
                                  h == 0, h == HALVES - 1)
                    last.then_inc(o_mm, 1)

            keep_warm(w1h[:, 0, 0:P], agg[:, 1, 1, :], WARM_NORM1)
            pe.wait_ge(ld_misc, 144)
            pe.wait_ge(z_cp, CHUNKS)
            turn_b(0)
            with pe.Fori(1, CHUNKS // UNROLL) as n:
                turn_b(n)

            pe.wait_ge(w_lo, CHUNKS)
            keep_warm(W[:, 0, 0, 0:P], W[:, 0, 0, 0:CH], WARM_NORM2)
            pe.wait_ge(o_cp, CHUNKS)

            def node_products(o, stat, mov, j, first):
                for b in range(CB):
                    at = slice(j * CH + b * P, j * CH + (b + 1) * P)
                    mm(o[:, b * P:(b + 1) * P], stat[:, 0, at], mov[:, 0, :], first, False)
                    mm(o[:, b * P:(b + 1) * P], stat[:, 0, at], mov[:, 1, :], False, False)
                    last = mm(o[:, b * P:(b + 1) * P], stat[:, 1, at], mov[:, 0, :], False, True)
                return last

            def input_products(g, u):
                t, prev = u.thread, before(u)
                if u == unit(1, 1, 0) and not (isinstance(g, int) and g == 0):
                    pe.wait_ge(h0l_d, chunk_no(g, GCH - 1))
                elif u.p == 1:
                    pe.wait_ge(h0l_d, chunk_no(g, u.c))
                elif u.p == 2 and u.s == 1:
                    pe.wait_ge(lo_p["x"], unit_no(g, unit(1, 1, 2 * u.c + 1)))
                elif u.p == 3 and u.s == 1:
                    pe.wait_ge(lo_p["x"], unit_no(g, unit(2, 2, u.c)))
                    if u.k == 0:
                        pe.wait_ge(y2_d, g * GCH + GCH)
                        pe.wait_ge(g_a["x"], g * X_GATES + X_GATES)
                elif u.p == 4 and u.s == 1:
                    pe.wait_ge(lo_p[t], unit_no(g, unit(3, 3, u.c, t)))
                src = opA if u.p == 1 else H[:, g % 2, :, :]
                for q in gates(u):
                    if u.k and q in gates(prev):
                        pe.wait_ge(g_a[t], gate_count(g, prev, q))
                    o = gate_bank(g, u, q)
                    at = (u.p - 1) * 4 * P + GATE[q] * P
                    w = [W[:, 0, part, at:at + P] for part in range(2)]
                    x = [windows(src[:, part, :], u, u.s - 1) for part in range(2)]
                    mm(o, w[0], x[0], True, False)
                    mm(o, w[1], x[0], False, False)
                    last = mm(o, w[0], x[1], False, u.s == 1)
                    if u.s == 1:
                        last.then_inc(g_t[t], 1)

            def hidden_products(g, u):
                t = u.thread
                before_no = unit_no(g, unit(u.p, u.s - 1, u.c, t))
                pe.wait_ge(hi_d[t], before_no)
                for n, q in enumerate(gates(u)):
                    o = gate_bank(g, u, q)
                    at = (u.p - 1) * 4 * P + GATE[q] * P
                    w = [W[:, 1, part, at:at + P] for part in range(2)]
                    h = [hst[t][:, u.c, part, 0:u.n] for part in range(2)]
                    mm(o, w[0], h[0], False, False)
                    mm(o, w[1], h[0], False, False)
                    if n == 0:
                        pe.wait_ge(lo_p[t], before_no)
                    mm(o, w[0], h[1], False, True).then_inc(g_t[t], 1)

            def turn_c(order, gw, gx, gy):
                for kind, j, _, g in steps(order, {"w": gw, "x": gx, "y": gy}):
                    if kind == "input":
                        input_products(g, j)
                        continue
                    if kind == "hidden":
                        hidden_products(g, j)
                        continue
                    if kind == "warm":
                        keep_warm(W[:, 0, 0, 0:P], W[:, 0, 0, 0:CH], j)
                        continue
                    o = ps[:, j, :]
                    if kind == "norm1":
                        if not (isinstance(g, int) and g == 0):
                            pe.wait_ge(rl_d, chunk_no(g - 1, j))
                        pe.wait_ge(yT_a, chunk_no(g, j))
                        for b in range(CB):
                            last = pe.transpose(o[:, b * P:(b + 1) * P], yT[:, j % 2, b * P:(b + 1) * P], ident)
                        last.then_inc(tr_t, 1)
                    elif kind == "agg1":
                        if not (isinstance(g, int) and g == 0):
                            pe.wait_ge(g_a["x"], gate_count(g - 1, unit(2, 2, 1), BANK_GATE[j]))
                        pe.wait_ge(x1h_a, chunk_no(g, j))
                        pe.wait_ge(x1l_p, chunk_no(g, j))
                        node_products(o, opA, adjh, j, True).then_inc(agg1_t, 1)
                    elif kind == "lin1":
                        pe.wait_ge(vl_d, chunk_no(g, j))
                        mm(o, bias1_w[:], bias1_x[:, :, :].rearrange("p b c -> p (b c)"), True, False)
                        mm(o, wgh[:, 0, 0, :], opB[:, 0, cols(j)], False, False)
                        mm(o, wgh[:, 0, 1, :], opB[:, 0, cols(j)], False, False)
                        mm(o, wgh[:, 0, 0, :], opB[:, 1, cols(j)], False, True).then_inc(lin1_t, 1)
                    elif kind == "lin2":
                        pe.wait_ge(rl_d, chunk_no(g, j))
                        if gw is not None:
                            pe.wait_ge(y_d, chunk_no(gw, j))
                        mm(o, bias2_w[:], bias2_x[:, :, :].rearrange("p b c -> p (b c)"), True, False)
                        node_products(o, opA, wgh[:, 1, :, :], j, False).then_inc(lin2_t, 1)
                    elif kind == "agg2":
                        pe.wait_ge(sl_d, chunk_no(g, j))
                        node_products(o, opB, adjh, j, True).then_inc(agg2_t, 1)
                    elif kind == "norm2":
                        o = ps[:, bank0["y"] + j, :]
                        t = "x" if late(g) else "y"
                        pe.wait_ge(lo_p[t], unit_no(g, unit(4, 4, j // 2, t)))
                        if late(g):
                            pe.wait_ge(y2_d, g * GCH + j + 1)
                        else:
                            pe.wait_ge(g_a[t], gate_count(g, unit(4, 4, 1, t), BANK_GATE[j]))
                        for b in range(CB):
                            at = slice(j * CH + b * P, j * CH + (b + 1) * P)
                            mm(o[:, b * P:(b + 1) * P], H[:, g % 2, 0, at], idh[:], True, False)
                            last = mm(o[:, b * P:(b + 1) * P], H[:, g % 2, 1, at], idh[:], False, True)
                        last.then_inc(fin_t, 1)

            turns(pe, turn_c, PE_ORDERS)

        @block.scalar
        def _(act):
            a = nc.scalar.activation

            act.wait_ge(ld_adj, 48)
            a(adjh[:, 0, :], adj_t, ACT.Copy, scale=WS).then_inc(pre_a, 1)
            act.wait_ge(ld_w1, 16)
            a(w1h[:, 0, :], w1, ACT.Copy, scale=WS).then_inc(pre_a, 1)

            def agg_high(n, i):
                k = n * UNROLL + i
                act.wait_ge(agg_mm, k + 1)
                if not (isinstance(k, int) and k < 2):
                    act.wait_ge(z_mm, k - 1)
                a(agg[:, i % 2, 0, :], ps[:, i % 2, :], ACT.Copy).then_inc(agg_hi, 1)

            def z_copy(n, i):
                k = n * UNROLL + i
                act.wait_ge(z_mm, k + 1)
                a(z[:, :, bass.ds(k * CH, CH)], ps[:, 2 + 2 * (i % 2):4 + 2 * (i % 2), :], ACT.Copy,
                  scale=1.0 / WS).then_inc(z_cp, 1)
                if isinstance(k, int) and k == 0:
                    act.wait_ge(ld_lstm, 32)
                s = bass.ds(k * WSL, WSL)
                a(W[:, :, 0, s], wst[:, :, s], ACT.Copy, scale=WS).then_inc(w_hi, 1)

            def turn_a(n):
                for i in range(UNROLL):
                    agg_high(n, i)
                    if not (isinstance(n, int) and i == 0):
                        z_copy(n, i - 1)

            turn_a(0)
            with act.Fori(1, CHUNKS // UNROLL) as n:
                turn_a(n)
            z_copy(CHUNKS // UNROLL, -1)

            act.wait_ge(ld_misc, 144)
            a(wgh[:, :, 0, :], wg, ACT.Copy, scale=WS).then_inc(pre_a, 1)
            a(idh[:], ident, ACT.Copy, scale=1.0 / HS).then_inc(pre_a, 1)

            act.wait_ge(bn1_d, 7)
            with act.Fori(0, CHUNKS // UNROLL) as n:
                for i in range(UNROLL):
                    for h in range(HALVES):
                        at = z[:, h, bass.ds(n * (UNROLL * CH) + i * CH, CH)]
                        a(at, at, ACT.Relu, bias=bn1[:, 3, h:h + 1], scale=bn1[:, 2, h:h + 1]).then_inc(r_act, 1)

            a(warm[:], ident[:, 0:1], ACT.Sigmoid)
            act.wait_ge(bn2_d, 7)

            def nonlinear(g, u, some):
                t = u.thread
                scale = 1.0 / (WS * (WS if u.p == 1 else HS))
                for q in some:
                    if u.k >= 3 and q == gates(u)[0]:
                        act.wait_ge(lo_p[t], g * UNITS[t] + (u.k - 2))
                    act.wait_ge(g_t[t], gate_count(g, u, q))
                    at = (u.p - 1) * 4 + GATE[q]
                    a(gate_buf(u, q), gate_bank(g, u, q), ACT.Tanh if q == "g" else ACT.Sigmoid,
                      bias=gbias[:, at:at + 1], scale=scale).then_inc(g_a[t], 1)

            def turn_c(order, gw, gx, gy):
                for kind, j, some, g in steps(order, {"w": gw, "x": gx, "y": gy}):
                    if kind == "gates":
                        nonlinear(g, j, some)
                    elif kind == "tanh":
                        t = j.thread
                        if j.s == 1:
                            act.wait_ge(c1_p[t], first_no(g, j))
                        else:
                            act.wait_ge(c_d[t], f_no(g, j))
                        a(gate_buf(j, "i"), cell[t][:, j.c % 2, 0:j.n], ACT.Tanh).then_inc(tc_a[t], 1)
                    elif kind == "yT":
                        if not (isinstance(g, int) and g == 0 and j < 2):
                            act.wait_ge(tr_t, g * GCH + (j - 1))
                        a(yT[:, j % 2, :], z[:, 0, bass.ds(g * GC + j * CH, CH)], ACT.Identity,
                          bias=bn2[:, 3, 0:1], scale=bn2[:, 2, 0:1]).then_inc(yT_a, 1)
                    elif kind == "apply1":
                        act.wait_ge(rs_p, g * (2 * GCH) + 2 * (j + 1))
                        if not (isinstance(g, int) and g < 3):
                            act.wait_ge(stored[j], g * 16 - 16)
                        for b in range(CB):
                            at = slice(b * P, (b + 1) * P)
                            last = a(x1[:, g % 3, j * CH + b * P:j * CH + (b + 1) * P], xin[:, j, at], ACT.Identity,
                                     bias=nmr[:, j, b:b + 1], scale=lrs["x"][:, j, b:b + 1])
                        last.then_inc(x1_a, 1)
                    elif kind == "applied":
                        act.wait_ge(x1_a, chunk_no(g, j))
                    elif kind == "x1":
                        a(opA[:, 0, cols(j)], x1[:, g % 3, cols(j)], ACT.Copy).then_inc(x1h_a, 1)
                    elif kind == "agg1":
                        act.wait_ge(agg1_t, chunk_no(g, j))
                        a(opB[:, 0, cols(j)], ps[:, j, :], ACT.Copy, scale=1.0 / WS).then_inc(vh_a, 1)
                    elif kind == "lin1":
                        act.wait_ge(lin1_t, chunk_no(g, j))
                        a(opA[:, 0, cols(j)], ps[:, j, :], ACT.Relu).then_inc(rh_a, 1)
                    elif kind == "lin2":
                        act.wait_ge(lin2_t, chunk_no(g, j))
                        a(opB[:, 0, cols(j)], ps[:, j, :], ACT.Copy, scale=1.0 / (WS * WS)).then_inc(sh_a, 1)
                    elif kind == "agg2":
                        act.wait_ge(agg2_t, chunk_no(g, j))
                        a(opA[:, 0, cols(j)], ps[:, j, :], ACT.Relu).then_inc(h0h_a, 1)

            turns(act, turn_c, ACT_ORDERS)

        @block.vector
        def _(dve):
            v = nc.vector

            dve.wait_ge(ld_adj, 48)
            v.tensor_tensor(tmp[:, 0, :], adj_n, ident, ALU.add).then_inc(pre_d, 1)
            v.tensor_tensor(tmp[:, 2, :], adj_t, ident, ALU.add).then_inc(pre_d, 1)
            dve.wait_ge(pre_d, 2)
            v.reduce_sum(sm[:, 0:1], tmp[:, 0, :], mybir.AxisListType.X)
            v.reduce_sum(sm[:, 1:2], tmp[:, 2, :], mybir.AxisListType.X)
            v.tensor_tensor(tmp[:, 3, :], tmp[:, 0, :], ident, ALU.mult).then_inc(pre_d, 1)
            dve.wait_ge(pre_d, 3)
            v.reduce_sum(sm[:, 2:3], tmp[:, 3, :], mybir.AxisListType.X)
            v.tensor_tensor(sm[:, 3:4], sm[:, 0:1], sm[:, 1:2], ALU.add).then_inc(pre_d, 1)
            dve.wait_ge(pre_d, 4)
            v.tensor_tensor(sm[:, 4:5], sm[:, 3:4], sm[:, 2:3], ALU.subtract).then_inc(pre_d, 1)
            dve.wait_ge(pre_p, 3)
            v.tensor_scalar(tmp[:, 1, :], tmp[:, 0, :], sm[:, 5:6], None, ALU.mult).then_inc(pre_d, 1)
            dve.wait_ge(pre_t, 2)
            v.tensor_scalar(ahat, ps[:, 0, 0:P], sm[:, 5:6], None, ALU.mult).then_inc(pre_d, 1)

            def low(o, full, high, scale):
                return v.scalar_tensor_tensor(out=o, in0=full, scalar=scale, in1=high, op0=ALU.mult, op1=ALU.subtract)

            dve.wait_ge(pre_a, 2)
            low(adjh[:, 1, :], adj_t, adjh[:, 0, :], WS)
            dve.wait_ge(ld_w1, 16)
            low(w1h[:, 1, :], w1, w1h[:, 0, :], WS).then_inc(w1_lo, 1)
            v.tensor_copy(tmp[:, 0, :], ps[:, 1, 0:P]).then_inc(pre_d, 1)

            def agg_low(n, i):
                dve.wait_ge(agg_hi, n * UNROLL + (i + 1))
                low(agg[:, i % 2, 1, :], ps[:, i % 2, :], agg[:, i % 2, 0, :], 1.0).then_inc(agg_lo, 1)

            def z_stats(n, i):
                k = n * UNROLL + i
                dve.wait_ge(w_hi, k + 1)
                dve.wait_ge(z_cp, k + 1)
                s = bass.ds(k * WSL, WSL)
                low(W[:, :, 1, s], wst[:, :, s], W[:, :, 0, s], WS).then_inc(w_lo, 1)
                for h in range(HALVES):
                    last = v.bn_stats(stats1[:, h, bass.ds(k, 1), :].rearrange("p a s -> p (a s)"),
                                      z[:, h, bass.ds(k * CH, CH)])
                last.then_inc(z_st, 1)

            def turn_a(n):
                for i in range(UNROLL):
                    agg_low(n, i)
                    if not (isinstance(n, int) and i < 2):
                        z_stats(n, i - 2)

            turn_a(0)
            with dve.Fori(1, CHUNKS // UNROLL) as n:
                turn_a(n)
            z_stats(CHUNKS // UNROLL, -2)
            z_stats(CHUNKS // UNROLL, -1)

            def batchnorm(stats_done, stats, mv, bn, vec, d, p):
                b, gamma, beta = vec
                dve.wait_ge(stats_done, CHUNKS)
                for h, st in enumerate(stats):
                    last = v.bn_aggr(mv[:, h, :], st)
                last.then_inc(d, 1)
                dve.wait_ge(d, 1)
                v.tensor_scalar(bn[:, 0, :], mv[:, :, 1], EPS, None, ALU.add).then_inc(d, 1)
                v.tensor_tensor(bn[:, 3, :], mv[:, :, 0], b, ALU.add).then_inc(d, 1)
                dve.wait_ge(d, 3)
                v.tensor_tensor(mv[:, :, 0], b, bn[:, 3, :], ALU.subtract).then_inc(d, 1)
                dve.wait_ge(p, 1)
                v.tensor_tensor(bn[:, 2, :], bn[:, 1, :], gamma, ALU.mult).then_inc(d, 1)
                dve.wait_ge(d, 5)
                v.tensor_tensor(bn[:, 1, :], mv[:, :, 0], bn[:, 2, :], ALU.mult).then_inc(d, 1)
                dve.wait_ge(d, 6)
                v.tensor_tensor(bn[:, 3, :], bn[:, 1, :], beta, ALU.add).then_inc(d, 1)

            dve.wait_ge(ld_misc, 144)
            batchnorm(z_st, [stats1[:, h, :, :].rearrange("p k s -> p (k s)") for h in range(HALVES)], mv1, bn1,
                      (v1[:, 0, :], v1[:, 1, :], v1[:, 2, :]), bn1_d, bn1_p)

            pick = cst[:, P:P + 8]
            dve.wait_ge(ld_misc, 144)
            v.tensor_scalar(tmp[:, 1, :], bgr[:, 0, :], WS, None, ALU.mult).then_inc(pre_d, 1)
            v.tensor_scalar(tmp[:, 2, :], bgr[:, 1, :], WS, None, ALU.mult).then_inc(pre_d, 1)
            v.tensor_tensor(gbias[:], bi[:, 0, :], bi[:, 1, :], ALU.add)
            at, done = 10, 10
            for src, dst, ph, pl, rep in ((tmp[:, 0, :], bias1_x, 0, 1, CB), (tmp[:, 1, :], bias1_w, 2, 3, 1),
                                          (tmp[:, 2, :], bias2_x, 4, 5, CB)):
                dve.wait_ge(pre_d, done)
                v.tensor_copy(tmph[:, 0, :], src).then_inc(pre_d, 1)
                dve.wait_ge(pre_d, done + 1)
                v.tensor_tensor(tmph[:, 1, :], src, tmph[:, 0, :], ALU.subtract).then_inc(pre_d, 1)
                v.tensor_scalar(tmp[:, 3, :], tmph[:, 0, :], pick[:, ph:ph + 1], None, ALU.mult).then_inc(pre_d, 1)
                dve.wait_ge(pre_d, done + 3)
                for b in range(rep):
                    o = dst[:, b, :] if rep > 1 else dst[:]
                    last = v.scalar_tensor_tensor(out=o, in0=tmph[:, 1, :], scalar=pick[:, pl:pl + 1],
                                                  in1=tmp[:, 3, :], op0=ALU.mult, op1=ALU.add)
                last.then_inc(pre_d, 1)
                done += 4
            dve.wait_ge(pre_p, 3)
            v.tensor_scalar(bias2_w[:], zero, pick[:, 6:7], WS, ALU.add, ALU.mult)
            dve.wait_ge(pre_a, 3)
            low(wgh[:, :, 1, :], wg, wgh[:, :, 0, :], WS)

            with dve.Fori(0, CHUNKS // UNROLL) as n:
                for i in range(UNROLL):
                    dve.wait_ge(o_mm, n * UNROLL + (i + 1))
                    v.tensor_scalar(z[:, 0, bass.ds(n * (UNROLL * CH) + i * CH, CH)], ps[:, i, :], 1.0, None, ALU.mult)
                    v.bn_stats(stats2[:, bass.ds(n * UNROLL + i, 1), :].rearrange("p a s -> p (a s)"),
                               ps[:, i, :]).then_inc(o_cp, 1)

            batchnorm(o_cp, [stats2[:, :, :].rearrange("p k s -> p (k s)")], mv2, bn2,
                      (v2[:, 0:1], v2[:, 1:2], v2[:, 2:3]), bn2_d, bn2_p)
            v.memset(mark[:, GCH:GCH + 1], 0.0).then_inc(y2_d, GCH)

            def norm_stats(t, g, y, j, y_s, y_done, st_s, mv_s):
                dve.wait_ge(y_s, y_done)
                for b in range(CB):
                    last = v.bn_stats(lst[t][:, j, b, :], y[:, b * P:(b + 1) * P])
                last.then_inc(st_s, 1)
                mean_e, m2_e, mean_o, m2_o = (lst[t][:, j, :, k] for k in (1, 2, 4, 5))
                mean, diff, m2, sq, ve = (lmv[t][:, j, k, :] for k in range(5))
                dve.wait_ge(st_s, chunk_no(g, j))
                v.tensor_tensor(diff, mean_e, mean_o, ALU.subtract)
                v.scalar_tensor_tensor(out=m2, in0=m2_e, scalar=P * EPS, in1=m2_o, op0=ALU.add,
                                       op1=ALU.add).then_inc(mv_s, 1)
                dve.wait_ge(mv_s, g * (3 * GCH) + (3 * j + 1))
                v.scalar_tensor_tensor(out=mean, in0=diff, scalar=-0.5 if t == "y" else 0.5, in1=mean_e, op0=ALU.mult,
                                       op1=ALU.add if t == "y" else ALU.subtract)
                v.scalar_tensor_tensor(out=sq, in0=diff, scalar=0.25, in1=diff, op0=ALU.mult,
                                       op1=ALU.mult).then_inc(mv_s, 1)
                dve.wait_ge(mv_s, g * (3 * GCH) + (3 * j + 2))
                v.scalar_tensor_tensor(out=ve, in0=m2, scalar=1.0 / P, in1=sq, op0=ALU.mult,
                                       op1=ALU.add).then_inc(mv_s, 1)

            def norm_apply(t, g, y, o, j, rs_s, o_s):
                dve.wait_ge(rs_s, chunk_no(g, j))
                for b in range(CB):
                    at = slice(b * P, (b + 1) * P)
                    last = v.tensor_scalar(o[:, at], y[:, at], lmv[t][:, j, 0, b:b + 1], lrs[t][:, j, b:b + 1],
                                           ALU.subtract, ALU.mult)
                last.then_inc(o_s, 1)

            def conv_low(g, j, high_s, o_s, o, scalar, op):
                dve.wait_ge(high_s, chunk_no(g, j))
                v.scalar_tensor_tensor(out=o[:, 1, cols(j)], in0=ps[:, j, :], scalar=scalar, in1=o[:, 0, cols(j)],
                                       op0=op, op1=ALU.subtract).then_inc(o_s, 1)

            def turn_c(order, gw, gx, gy):
                for kind, j, _, g in steps(order, {"w": gw, "x": gx, "y": gy}):
                    if kind == "ig":
                        u, t = j, j.thread
                        dve.wait_ge(g_a[t], gate_count(g, u, "g"))
                        v.tensor_tensor(gate_buf(u, "g"), gate_buf(u, "i"), gate_buf(u, "g"),
                                        ALU.mult).then_inc(ig_d[t], 1)
                    elif kind == "cell":
                        u, t = j, j.thread
                        dve.wait_ge(ig_d[t], f_no(g, u))
                        dve.wait_ge(fc_p[t], f_no(g, u))
                        v.tensor_tensor(cell[t][:, u.c % 2, 0:u.n], gate_buf(u, "g"), gate_buf(u, "f"),
                                        ALU.add).then_inc(c_d[t], 1)
                    elif kind == "h":
                        u, t = j, j.thread
                        dve.wait_ge(g_a[t], gate_count(g, u, "o"))
                        dve.wait_ge(tc_a[t], unit_no(g, u))
                        v.scalar_tensor_tensor(out=gate_buf(u, "g"), in0=gate_buf(u, "o"), scalar=HS,
                                               in1=gate_buf(u, "i"), op0=ALU.mult, op1=ALU.mult).then_inc(h_d[t], 1)
                        dve.wait_ge(h_d[t], unit_no(g, u))
                        v.tensor_copy(h_out(g, u, 0), folded(gate_buf(u, "g"), u)).then_inc(hi_d[t], 1)
                    elif kind == "sum1":
                        dve.wait_ge(tr_t, chunk_no(g, j))
                        dve.wait_ge(ld_xin[j], g * 16 + 16)
                        v.tensor_tensor(xin[:, j, :], ps[:, j, :], xin[:, j, :], ALU.add).then_inc(y_d, 1)
                    elif kind == "stats1":
                        norm_stats("x", g, xin[:, j, :], j, y_d, chunk_no(g, j), st_d, mv_d)
                    elif kind == "agg1":
                        conv_low(g, j, vh_a, vl_d, opB, 1.0 / WS, ALU.mult)
                    elif kind == "lin1":
                        conv_low(g, j, rh_a, rl_d, opA, 0.0, ALU.max)
                    elif kind == "lin2":
                        conv_low(g, j, sh_a, sl_d, opB, 1.0 / (WS * WS), ALU.mult)
                    elif kind == "agg2":
                        conv_low(g, j, h0h_a, h0l_d, opA, 0.0, ALU.max)
                    elif kind == "sum2":
                        dve.wait_ge(fin_t, chunk_no(g, j))
                        if j >= 2:
                            dve.wait_ge(o_d, chunk_no(g, j - 2))
                        elif isinstance(g, int):
                            dve.wait_ge(o_d, chunk_no(g - 1, j + 2))
                        v.tensor_tensor(y2[:, j % 2, :], ps[:, bank0["y"] + j, :], x1[:, g % 3, cols(j)],
                                        ALU.add).then_inc(y2_d, 1)
                    elif kind == "stats2":
                        norm_stats("y", g, y2[:, j % 2, :], j, y2_d, g * GCH + (GCH + j + 1), st2_d, mv2_d)
                    elif kind == "store":
                        norm_apply("y", g, y2[:, j % 2, :], x1[:, g % 3, cols(j)], j, rs2_p, o_d)

            turns(dve, turn_c, DVE_ORDERS)

        @block.gpsimd
        def _(pool):
            gp = nc.gpsimd
            gp.memset(minus_half[:], -0.5).then_inc(pre_p, 1)
            gp.memset(zero, 0.0)
            for j in range(GCH):
                gp.memset(mark[:, j:j + 1], 0.0).then_inc(stored[j], 16)
            gp.memset(ones, 1.0).then_inc(pre_p, 1)
            pool.wait_ge(pre_p, 2)
            pool.wait_ge(pre_d, 5)
            gp.tensor_tensor(sm[:, 5:6], sm[:, 4:5], minus_half[:, 0:1], ALU.pow).then_inc(pre_p, 1)
            for bn, h, d, p in ((bn1, HALVES, bn1_d, bn1_p), (bn2, 1, bn2_d, bn2_p)):
                pool.wait_ge(d, 2)
                gp.tensor_tensor(bn[:, 1, :], bn[:, 0, :], minus_half[:, 0:h], ALU.pow).then_inc(p, 1)

            def rstd(t, g, j, mv_s, rs_s):
                pool.wait_ge(mv_s, g * (3 * GCH) + 3 * (j + 1))
                gp.tensor_tensor(lrs[t][:, j, :], lmv[t][:, j, 4, :], minus_half[:], ALU.pow).then_inc(rs_s, 1)
                if t == "x":
                    pool.wait_ge(rs_s, g * (2 * GCH) + (2 * j + 1))
                    gp.tensor_tensor(nmr[:, j, :], lmv[t][:, j, 0, :], lrs[t][:, j, :], ALU.mult).then_inc(rs_s, 1)

            def turn_c(order, gw, gx, gy):
                for kind, j, _, g in steps(order, {"w": gw, "x": gx, "y": gy}):
                    if kind == "c1":
                        u, t = j, j.thread
                        pool.wait_ge(g_a[t], gate_count(g, u, "g"))
                        gp.tensor_tensor(cell[t][:, u.c % 2, 0:u.n], gate_buf(u, "i"), gate_buf(u, "g"),
                                         ALU.mult).then_inc(c1_p[t], 1)
                    elif kind == "fc":
                        u, t = j, j.thread
                        pool.wait_ge(g_a[t], gate_count(g, u, "f"))
                        gp.tensor_tensor(gate_buf(u, "f"), gate_buf(u, "f"), cell[t][:, u.c % 2, 0:u.n],
                                         ALU.mult).then_inc(fc_p[t], 1)
                    elif kind == "h":
                        u, t = j, j.thread
                        pool.wait_ge(hi_d[t], unit_no(g, u))
                        gp.tensor_tensor(h_out(g, u, 1), folded(gate_buf(u, "g"), u), h_out(g, u, 0),
                                         ALU.subtract).then_inc(lo_p[t], 1)
                    elif kind == "rstd1":
                        rstd("x", g, j, mv_d, rs_p)
                    elif kind == "x1":
                        pool.wait_ge(x1h_a, chunk_no(g, j))
                        gp.tensor_tensor(opA[:, 1, cols(j)], x1[:, g % 3, cols(j)], opA[:, 0, cols(j)],
                                         ALU.subtract).then_inc(x1l_p, 1)
                    elif kind == "rstd2":
                        rstd("y", g, j, mv2_d, rs2_p)

            turns(pool, turn_c, POOL_ORDERS)


def kernel(**inputs):
    import numpy as _np
    import concourse.bacc as _bacc
    from concourse import mybir as _mybir
    from concourse.bass_utils import run_bass_kernel_spmd as _run

    a = {k: _np.asarray(v) for k, v in inputs.items()}

    def column(v, n):
        return v.reshape(n, P).T

    consts = _np.zeros((P, P + 8), _np.float32)
    consts[:, :P] = _np.eye(P)
    for c, rows in enumerate(((0, 2), (1, 3), (0, 1), (2, 3), (0,), (1,), (0, 1))):
        consts[list(rows), P + c] = 1.0

    host = {
        "xn": a["x"].transpose(1, 0, 2).reshape(P, COLS),
        "adj": a["adj"],
        "adjT": a["adj"].T,
        "W1T": a["L0_gnn_W1"].T,
        "W2T": a["L0_gnn_W2"].T.reshape(HALVES, P, P).transpose(1, 0, 2),
        "vec1": _np.stack([column(a[f"L0_gnn_{n}"], HALVES) for n in ("b1", "g1", "be1")], 1),
        "vec2": _np.stack([a[f"L0_gnn_{n}"] for n in ("b2", "g2", "be2")], 1),
        "Wg0": a["L1_gnn_Wg0"],
        "Wg1": a["L1_gnn_Wg1"],
        "bg0": _np.broadcast_to(a["L1_gnn_bg0"], (P, P)),
        "bg1": _np.broadcast_to(a["L1_gnn_bg1"], (P, P)),
        "WihT": a["L1_gnn_Wih"].transpose(2, 0, 1).reshape(P, -1),
        "WhhT": a["L1_gnn_Whh"].transpose(2, 0, 1).reshape(P, -1),
        "bih": column(a["L1_gnn_bih"].reshape(-1), MAX_SKIP * 4),
        "bhh": column(a["L1_gnn_bhh"].reshape(-1), MAX_SKIP * 4),
        "consts": consts,
    }
    nc = _bacc.Bacc("TRN2", target_bir_lowering=False, num_devices=1)
    arrays, args = {}, []
    for name, v in host.items():
        v = _np.ascontiguousarray(v)
        arrays[f"in_{name}_dram"] = v
        args.append(nc.dram_tensor(f"in_{name}_dram", v.shape, _mybir.dt.from_np(v.dtype), kind="ExternalInput").ap())
    args.append(nc.dram_tensor("out_dram", (P, COLS), F32, kind="ExternalOutput").ap())
    gnn_kernel(nc, *args)
    r = _run(nc, [arrays], core_ids=[0])
    got = r.results[0]["out_dram"]
    return _np.ascontiguousarray(got.reshape(P, B, P).transpose(1, 0, 2))
```
